# Optimizing a Trainium2 kernel written in Bass

```python
import numpy as np
import jax
import jax.numpy as jnp

def _softmax(x, axis=-1):
    return jax.nn.softmax(x, axis=axis)

def _gelu(x):
    return jax.nn.gelu(x, approximate=True)

def _silu(x):
    return jax.nn.silu(x)

def _sigmoid(x):
    return jax.nn.sigmoid(x)

def _layernorm(x, axis=-1, eps=1e-05):
    m = jnp.mean(x, axis=axis, keepdims=True)
    v = jnp.var(x, axis=axis, keepdims=True)
    return (x - m) / jnp.sqrt(v + eps)

def _scatter_add(tgt, idx, src, axis=0):
    return tgt.at[idx].add(src)

def _segment_sum(src, seg, n):
    return jax.ops.segment_sum(src, seg, n)
kernel_name = 'mk_adj_preln_d2_adj_r2_f49381'

def setup_inputs(seed: int=0):
    np.random.seed(seed)
    _w = jnp.asarray

    def _rec_inputs():
        import jax
        import jax.numpy as jnp
        _gk = jax.random.key(seed)
        x = -0.0005207 + 1.001 * jax.random.normal(jax.random.fold_in(_gk, 1), (2048, 256), jnp.float32)
        _a = jax.random.bernoulli(jax.random.fold_in(_gk, 2), 0.00390625, (2048, 2048))
        adj = _a.astype(jnp.int32)
        return (x, adj)
    x, adj = _rec_inputs()

    def _L0_gnn_setup():
        import jax, jax.numpy as jnp
        import numpy as np
        N = 2048
        STATE_DIM = 256
        OUTPUT_DIM = 256
        N_STEPS = 5
        W_STD = 0.02

        def _lin_params(key, out_dim, in_dim):
            W = jax.random.normal(key, (out_dim, in_dim), dtype=jnp.float32) * W_STD
            b = jnp.zeros((out_dim,), dtype=jnp.float32)
            return (W, b)
        key = jax.random.key(seed)
        ks = jax.random.split(key, 10)
        prop_state = jax.random.normal(ks[0], (N, STATE_DIM), dtype=jnp.float32)
        A = jax.random.randint(ks[1], (N, N), 0, 2, dtype=jnp.int64)
        in_W, in_b = _lin_params(ks[2], STATE_DIM, STATE_DIM)
        out_W, out_b = _lin_params(ks[3], STATE_DIM, STATE_DIM)
        r_W, r_b = _lin_params(ks[4], STATE_DIM, 3 * STATE_DIM)
        z_W, z_b = _lin_params(ks[5], STATE_DIM, 3 * STATE_DIM)
        h_W, h_b = _lin_params(ks[6], STATE_DIM, 3 * STATE_DIM)
        o1_W, o1_b = _lin_params(ks[7], STATE_DIM, STATE_DIM)
        o2_W, o2_b = _lin_params(ks[8], OUTPUT_DIM, STATE_DIM)
        return {'prop_state': prop_state, 'A': A, 'in_W': in_W, 'in_b': in_b, 'out_W': out_W, 'out_b': out_b, 'r_W': r_W, 'r_b': r_b, 'z_W': z_W, 'z_b': z_b, 'h_W': h_W, 'h_b': h_b, 'o1_W': o1_W, 'o1_b': o1_b, 'o2_W': o2_W, 'o2_b': o2_b}
    _L0_gnn_all = _L0_gnn_setup()
    _L0_gnn_in = {k: v for k, v in _L0_gnn_all.items() if k in ('in_W', 'in_b', 'out_W', 'out_b', 'r_W', 'r_b', 'z_W', 'z_b', 'h_W', 'h_b', 'o1_W', 'o1_b', 'o2_W', 'o2_b')}
    del _L0_gnn_all

    def _L1_gnn_setup():
        import jax, jax.numpy as jnp
        import numpy as np
        N = 4096
        D_IN = 256
        D_OUT = 256
        key = jax.random.key(seed)
        k1, k2, k3, k4 = jax.random.split(key, 4)
        node_feats = jax.random.normal(k1, (N, D_IN), dtype=jnp.float32)
        adj_matrix = jax.random.randint(k2, (N, N), 0, 2, dtype=jnp.int32)
        w_self = jax.random.normal(k3, (D_OUT, D_IN), dtype=jnp.float32) * D_IN ** (-0.5)
        w_neigh = jax.random.normal(k4, (D_OUT, D_IN), dtype=jnp.float32) * D_IN ** (-0.5)
        return {'node_feats': node_feats, 'adj_matrix': adj_matrix, 'w_self': w_self, 'w_neigh': w_neigh}
    _L1_gnn_all = _L1_gnn_setup()
    _L1_gnn_in = {k: v for k, v in _L1_gnn_all.items() if k in ('w_self', 'w_neigh')}
    del _L1_gnn_all
    return {'x': x, 'adj': adj, 'L0_gnn_in_W': _L0_gnn_in['in_W'], 'L0_gnn_in_b': _L0_gnn_in['in_b'], 'L0_gnn_out_W': _L0_gnn_in['out_W'], 'L0_gnn_out_b': _L0_gnn_in['out_b'], 'L0_gnn_r_W': _L0_gnn_in['r_W'], 'L0_gnn_r_b': _L0_gnn_in['r_b'], 'L0_gnn_z_W': _L0_gnn_in['z_W'], 'L0_gnn_z_b': _L0_gnn_in['z_b'], 'L0_gnn_h_W': _L0_gnn_in['h_W'], 'L0_gnn_h_b': _L0_gnn_in['h_b'], 'L0_gnn_o1_W': _L0_gnn_in['o1_W'], 'L0_gnn_o1_b': _L0_gnn_in['o1_b'], 'L0_gnn_o2_W': _L0_gnn_in['o2_W'], 'L0_gnn_o2_b': _L0_gnn_in['o2_b'], 'L1_gnn_w_self': _L1_gnn_in['w_self'], 'L1_gnn_w_neigh': _L1_gnn_in['w_neigh']}

def reference(x, adj, L0_gnn_in_W, L0_gnn_in_b, L0_gnn_out_W, L0_gnn_out_b, L0_gnn_r_W, L0_gnn_r_b, L0_gnn_z_W, L0_gnn_z_b, L0_gnn_h_W, L0_gnn_h_b, L0_gnn_o1_W, L0_gnn_o1_b, L0_gnn_o2_W, L0_gnn_o2_b, L1_gnn_w_self, L1_gnn_w_neigh):
    import jax
    import jax.numpy as jnp

    def _L0_gnn_ref(prop_state, A, in_W, in_b, out_W, out_b, r_W, r_b, z_W, z_b, h_W, h_b, o1_W, o1_b, o2_W, o2_b):
        import jax, jax.numpy as jnp
        import numpy as np
        N = 2048
        STATE_DIM = 256
        OUTPUT_DIM = 256
        N_STEPS = 5
        W_STD = 0.02

        def _lin_params(key, out_dim, in_dim):
            W = jax.random.normal(key, (out_dim, in_dim), dtype=jnp.float32) * W_STD
            b = jnp.zeros((out_dim,), dtype=jnp.float32)
            return (W, b)
        Af = A.astype(prop_state.dtype)
        AfT = Af.T
        state = prop_state
        for _ in range(N_STEPS):
            s_in = state @ in_W.T + in_b
            s_out = state @ out_W.T + out_b
            a_in = Af @ s_in
            a_out = AfT @ s_out
            a = jnp.concatenate([a_in, a_out, state], axis=-1)
            r = jax.nn.sigmoid(a @ r_W.T + r_b)
            z = jax.nn.sigmoid(a @ z_W.T + z_b)
            joined = jnp.concatenate([a_in, a_out, r * state], axis=-1)
            h_hat = jnp.tanh(joined @ h_W.T + h_b)
            state = (1.0 - z) * state + z * h_hat
        out = jnp.tanh(state @ o1_W.T + o1_b) @ o2_W.T + o2_b
        return out

    def _L1_gnn_ref(node_feats, adj_matrix, w_self, w_neigh):
        import jax, jax.numpy as jnp
        import numpy as np
        N = 4096
        D_IN = 256
        D_OUT = 256
        adj_f = adj_matrix.astype(node_feats.dtype)
        s = adj_f @ node_feats[:, 0]
        has_neigh = jnp.sum(adj_matrix, axis=1) > 0
        s = jnp.where(has_neigh, s, jnp.zeros_like(s))
        neigh_term = s[:, None] * jnp.sum(w_neigh, axis=1)[None, :]
        return jax.nn.relu(node_feats @ w_self.T + neigh_term)
    h = jnp.maximum(_layernorm(x, axis=-1), 0.0)
    x = x + _L0_gnn_ref(h, adj, L0_gnn_in_W, L0_gnn_in_b, L0_gnn_out_W, L0_gnn_out_b, L0_gnn_r_W, L0_gnn_r_b, L0_gnn_z_W, L0_gnn_z_b, L0_gnn_h_W, L0_gnn_h_b, L0_gnn_o1_W, L0_gnn_o1_b, L0_gnn_o2_W, L0_gnn_o2_b)
    h = jnp.maximum(_layernorm(x, axis=-1), 0.0)
    x = x + _L1_gnn_ref(h, adj, L1_gnn_w_self, L1_gnn_w_neigh)
    return x

_drawn_inputs = setup_inputs


def setup_inputs(seed=0):
    import zlib

    import numpy as np

    out = dict(_drawn_inputs(seed))
    spreads = {'L0_gnn_in_b': (0.0, 0.1),
     'L0_gnn_out_b': (0.0, 0.1),
     'L0_gnn_r_b': (0.0, 0.8),
     'L0_gnn_z_b': (0.0, 0.8),
     'L0_gnn_h_b': (0.0, 0.609),
     'L0_gnn_o1_b': (0.0, 0.1),
     'L0_gnn_o2_b': (0.0, 0.1)}
    factors = {'L0_gnn_in_W': 2.928, 'L0_gnn_r_W': 8.0, 'L0_gnn_z_W': 8.0}
    for name, (base, spread) in spreads.items():
        noise = np.random.default_rng([zlib.crc32(name.encode()), seed]).standard_normal(out[name].shape)
        drawn = base * np.exp(spread * noise) if base else spread * noise
        out[name] = jnp.asarray(drawn.astype(out[name].dtype))
    for name, factor in factors.items():
        out[name] = (out[name] * factor).astype(out[name].dtype)
    return out
```

```python
from contextlib import ExitStack

import concourse.bass as bass
from concourse import mybir

ALU = mybir.AluOpType
ACT = mybir.ActivationFunctionType
AX = mybir.AxisListType
F32 = mybir.dt.float32
F16 = mybir.dt.float16
I32 = mybir.dt.int32

P = 128
N = 2048
D = 256
STEPS = 5
TILES = N // P
CHUNK = 512
CHUNKS = N // CHUNK
PER_CHUNK = CHUNK // P
FT = D // P
KT = 3 * FT
UNITS = 3 * FT
R, Z, H = 0, 1, 2
HI, LO = 0, 1
EPS = 1e-5
STATE_SCALE = 2.0 ** 11
EXP_MASK = 0x7F800000
MANT = 2.0 ** 23


def gnn_kernel(nc, x, adj, in_W, in_b, out_W, out_b, r_W, r_b, z_W, z_b, h_W, h_b,
               o1_W, o1_b, o2_W, o2_b, w_self, w_neigh, out):
    ctx = ExitStack()
    with ctx:
        ctx.enter_context(nc.allow_non_contiguous_dma(reason="biases as columns, 256 numbers each"))

        def sb(name, shape, dt):
            return ctx.enter_context(nc.sbuf_tensor(name, shape, dt))

        def sem(name):
            return ctx.enter_context(nc.semaphore(name))

        A16 = sb("A16", [P, TILES, N], F16)
        AT16 = sb("AT16", [P, TILES, TILES, P], F16)
        state_n = sb("state_n", [P, 2, TILES, D], F16)
        state_t = sb("state_t", [P, FT, N], F32)
        W16 = sb("W16", [P, 2, 3, KT, D], F16)
        deg_in = sb("deg_in", [P, N], F16)
        deg_out = sb("deg_out", [P, N], F16)
        work = sb("work", [P, 18 * 512], F16)
        ident = sb("ident", [P, P], F32)
        ident16 = sb("ident16", [P, P], F16)
        ones16 = sb("ones16", [P, P], F16)
        rowmax = sb("rowmax", [P, UNITS], F32)
        sigma = sb("sigma", [P, UNITS], F32)
        c_gate = sb("c_gate", [P, UNITS, 2], F32)
        gate_b = sb("gate_b", [P, UNITS], F32)
        inv = sb("inv", [P, UNITS], F32)
        o1b = sb("o1b", [P, FT], F32)
        deg_col = sb("deg_col", [P, TILES], F32)
        stats = sb("stats", [P, PER_CHUNK, 6], F32)
        mv = sb("mv", [P, TILES, 2], F32)
        sd = sb("sd", [P, TILES], F32)
        rstd = sb("rstd", [P, TILES], F32)
        tmp = sb("tmp", [P, TILES], F32)
        dmax = sb("dmax", [P, 2], F32)
        k_scale = sb("k_scale", [P, 1], F32)
        u_scale = sb("u_scale", [P, 1], F32)
        h2col = sb("h2col", [P, TILES, 2], F16)
        s_col = sb("s_col", [P, TILES], F32)

        uv = work[:, 0:5 * 1024].rearrange("p (s h n) -> p s h n", s=5, h=2)
        ss = work[:, 5 * 1024:7 * 1024].rearrange("p (h f n) -> p h f n", h=2, f=FT)
        zt = work[:, 7 * 1024:9 * 1024].bitcast(F32).rearrange("p (f n) -> p f n", f=FT)
        a_in = work[:, 0:8 * 1024].bitcast(I32).rearrange("p (b n) -> p b n", b=2)
        xs = A16[:, TILES - 4:TILES, :].rearrange("p a n -> p (a n)").bitcast(F32).rearrange("p (t d) -> p t d", d=D)
        tail = AT16[:, 9:16, :, :].rearrange("p a b c -> p (a b c)").bitcast(F32)
        wst = tail[:, 0:UNITS * 3 * D].rearrange("p (u k) -> p u k", u=UNITS)
        o = UNITS * 3 * D
        DB = D + 1
        inw = tail[:, o:o + 2 * FT * DB].rearrange("p (s k n) -> p s k n", s=2, k=FT)
        o += 2 * FT * DB
        wt = tail[:, o:o + 2 * 4 * P].rearrange("p (b k n) -> p b k n", b=2, k=4)
        late = A16[:, :, :].rearrange("p a n -> p (a n)").bitcast(F32)
        xr = late[:, 0:4096].rearrange("p (t d) -> p t d", d=D)
        x1 = late[:, 4096:8192].rearrange("p (t d) -> p t d", d=D)
        h2 = late[:, 8192:12288].rearrange("p (t d) -> p t d", d=D)
        head_n = late[:, 12288:14336].rearrange("p (w g d) -> p w g d", w=4, g=FT)
        head_t = late[:, 14336:15872].rearrange("p (w k d) -> p w k d", w=3, k=FT)
        o2b_all = late[:, 15872:16128]
        wsum_all = late[:, 16128:16384]
        neigh_t = work[:, 0:1024].bitcast(F32).rearrange("p (k d) -> p k d", k=FT)
        ones32 = work[:, 1024:1280].bitcast(F32)
        th = state_n[:, :, :, :].rearrange("p h t d -> p (h t d)").bitcast(F32).rearrange("p (g n) -> p g n", g=FT)
        h2t = state_t

        bank = [ctx.enter_context(nc.psum_tensor(f"bank{i}", [P, CHUNK], F32)) for i in range(8)]

        x_loaded = [sem(f"x_loaded{c}") for c in range(CHUNKS)]
        weights_loaded = sem("weights_loaded")
        adj_loaded = [sem(f"adj_loaded{b}") for b in range(2)]
        ident_zeroed = sem("ident_zeroed")
        ident_ready = sem("ident_ready")
        ident16_ready = sem("ident16_ready")
        adj_cast = sem("adj_cast")
        deg_added = sem("deg_added")
        adj_turned = sem("adj_turned")
        adj_t_ready = sem("adj_t_ready")
        w_turned = sem("w_turned")
        wt_ready = sem("wt_ready")
        w_combined = sem("w_combined")
        cw_ready = sem("cw_ready")
        w_scaled = sem("w_scaled")
        w_rows_turned = sem("w_rows_turned")
        w_hi = sem("w_hi")
        w_split = sem("w_split")
        dve_chain = sem("dve_chain")
        var_ready = sem("var_ready")
        sd_ready = sem("sd_ready")
        h0_ready = sem("h0_ready")
        h0_hi = sem("h0_hi")
        x_turned = sem("x_turned")
        diag_ready = sem("diag_ready")
        deg_summed = sem("deg_summed")
        deg_ready = sem("deg_ready")
        scales_ready = sem("scales_ready")

        uv_summed = sem("uv_summed")
        uv_hi = sem("uv_hi")
        uv_split = sem("uv_split")
        uv_used = sem("uv_used")
        s_hi = sem("s_hi")
        s_split = sem("s_split")
        gate_summed = sem("gate_summed")
        gate_biased = sem("gate_biased")
        gate_on = sem("gate_on")
        rs_ready = sem("rs_ready")
        rs_hi = sem("rs_hi")
        rs_split = sem("rs_split")
        state_new = sem("state_new")
        turned = sem("turned")
        node_hi = sem("node_hi")
        node_split = sem("node_split")
        step_chain = sem("step_chain")

        xr_loaded = sem("xr_loaded")
        head_loaded = sem("head_loaded")
        ones_ready = sem("ones_ready")
        xb_ready = sem("xb_ready")
        head_turned = sem("head_turned")
        head_ready = sem("head_ready")
        wsum_summed = sem("wsum_summed")
        wsum_ready = sem("wsum_ready")
        th_summed = sem("th_summed")
        th_ready = sem("th_ready")
        o2_summed = sem("o2_summed")
        o2_taken = sem("o2_taken")
        var2_ready = sem("var2_ready")
        sd2_ready = sem("sd2_ready")
        h2_ready = sem("h2_ready")
        h2_turned = sem("h2_turned")
        h2t_ready = sem("h2t_ready")
        h2col_ready = sem("h2col_ready")
        s_summed = sem("s_summed")
        s_ready = sem("s_ready")
        self_summed = sem("self_summed")
        self_taken = sem("self_taken")
        out_ready = sem("out_ready")
        stored = sem("stored")

        N_WEIGHT_DMAS = 3 + 2 + 2 + 3 + 1

        def chunk_of(c):
            return slice(c * CHUNK, (c + 1) * CHUNK)

        def adj_moving(g, jt, c):
            if g < FT:
                return AT16[:, PER_CHUNK * c:PER_CHUNK * (c + 1), jt, :]
            return A16[:, jt, chunk_of(c)]

        def uv_slot(c, g):
            return c % 2 if g == 0 else g + 1

        GROUPS = [(Z, 0, 4), (Z, 1, 5), (R, 0, 6), (R, 1, 7), (H, 0, 4), (H, 1, 5)]
        G = len(GROUPS)
        UV = 2 * FT
        TURNS = [(3, 6, 7), (0, 0, 1), (1, 2, 3), (2, 0, 1)]

        block = ctx.enter_context(nc.Block())

        @block.sync
        def _(sp):
            for it in range(TILES):
                if it >= 2:
                    sp.wait_ge(adj_cast, it - 1)
                sp.dma_start(a_in[:, it % 2, :], adj[it * P:(it + 1) * P, :]).then_inc(adj_loaded[it % 2], 16)
            sp.wait_ge(uv_summed, STEPS * CHUNKS * UV)
            for w, src in enumerate((o1_W, o2_W, w_self, w_neigh)):
                sp.dma_start(head_n[:, w, :, :], src.rearrange("(g p) d -> p g d", p=P)).then_inc(head_loaded, 16)
            sp.dma_start(o2b_all, o2_b.rearrange("(a d) -> a d", a=1).broadcast_to([P, D])).then_inc(head_loaded, 16)
            for c in range(CHUNKS):
                sp.dma_start(xr[:, 4 * c:4 * c + 4, :],
                             x[chunk_of(c), :].rearrange("(t p) d -> p t d", p=P)).then_inc(xr_loaded, 16)
            for c in range(CHUNKS):
                sp.wait_ge(out_ready, 4 * (c + 1))
                sp.dma_start(out[chunk_of(c), :].rearrange("(t p) d -> p t d", p=P),
                             x1[:, 4 * c:4 * c + 4, :]).then_inc(stored, 16)
            sp.wait_ge(stored, 16 * CHUNKS)

        @block.gpsimd
        def _(pool):
            nc.gpsimd.memset(ident[:, :], 0.0).then_inc(ident_zeroed, 1)
            nc.gpsimd.memset(ones16[:, :], 1.0)
            pool.wait_ge(ident_zeroed, 1)
            nc.gpsimd.affine_select(out=ident[:, :], in_=ident[:, :], compare_op=ALU.not_equal, fill=1.0,
                                    base=0, pattern=[[-1, P]], channel_multiplier=1).then_inc(ident_ready, 1)
            pool.wait_ge(ident_ready, 1)
            nc.gpsimd.tensor_copy(ident16[:, :], ident[:, :]).then_inc(ident16_ready, 1)
            for it in range(TILES):
                pool.wait_ge(adj_cast, it + 1)
                if it == 0:
                    nc.gpsimd.tensor_copy(deg_out[:, :], A16[:, 0, :]).then_inc(deg_added, 1)
                else:
                    pool.wait_ge(deg_added, it)
                    nc.gpsimd.tensor_tensor(deg_out[:, :], deg_out[:, :], A16[:, it, :],
                                            ALU.add).then_inc(deg_added, 1)
            pool.wait_ge(uv_summed, STEPS * CHUNKS * UV)
            pool.wait_ge(uv_used, STEPS * CHUNKS)
            nc.gpsimd.memset(ones32, 1.0).then_inc(ones_ready, 1)
            pool.wait_ge(head_loaded, 16 * 5)
            pool.wait_ge(xr_loaded, 16 * CHUNKS)
            for t in range(TILES):
                nc.gpsimd.tensor_tensor(xr[:, t, :], xr[:, t, :], o2b_all, ALU.add).then_inc(xb_ready, 1)

        @block.scalar
        def _(act):
            for q, src in enumerate((r_W, z_W, h_W)):
                act.dma_start(wst[:, 2 * q:2 * q + 2, :],
                              src.rearrange("(m p) k -> p m k", p=P)).then_inc(weights_loaded, 16)
            for s, (src, b) in enumerate(((in_W, in_b), (out_W, out_b))):
                act.dma_start(inw[:, s, :, 0:D], src.rearrange("(k p) d -> p k d", p=P)).then_inc(weights_loaded, 16)
                act.dma_start(inw[:, s, :, D:DB],
                              b.rearrange("(k p a) -> p k a", p=P, a=1)).then_inc(weights_loaded, 16)
            for q, src in enumerate((r_b, z_b, h_b)):
                act.dma_start(gate_b[:, 2 * q:2 * q + 2], src.rearrange("(m p) -> p m", p=P)).then_inc(weights_loaded, 16)
            act.dma_start(o1b[:, :], o1_b.rearrange("(m p) -> p m", p=P)).then_inc(weights_loaded, 16)
            for c in range(CHUNKS):
                act.dma_start(xs[:, 4 * c:4 * c + 4, :],
                              x[chunk_of(c), :].rearrange("(t p) d -> p t d", p=P)).then_inc(x_loaded[c], 16)

            for it in range(TILES):
                act.wait_ge(adj_loaded[it % 2], 16 * (it // 2 + 1))
                if it == TILES - 4:
                    act.wait_ge(x_turned, 2 * CHUNKS)
                    act.wait_ge(node_split, 2 * (CHUNKS - 1))
                nc.scalar.activation(A16[:, it, :], a_in[:, it % 2, :], ACT.Copy,
                                     accum_out=deg_col[:, it:it + 1]).then_inc(adj_cast, 1)
                u = it - 1
                if 0 <= u < UNITS:
                    act.wait_ge(w_combined, u + 1)
                    nc.scalar.activation(wst[:, u, 0:D], bank[3][:, 0:D], ACT.Copy)
                    nc.scalar.activation(wst[:, u, D:2 * D], bank[4][:, 0:D], ACT.Copy)
                    nc.scalar.activation(c_gate[:, u, 0:1], bank[3][:, D:DB], ACT.Copy)
                    nc.scalar.activation(c_gate[:, u, 1:2], bank[4][:, D:DB], ACT.Copy).then_inc(cw_ready, 1)
                u = it - 2
                if 0 <= u < UNITS:
                    q, m = divmod(u, FT)
                    act.wait_ge(w_rows_turned, u + 1)
                    cols = slice(m * P, (m + 1) * P)
                    nc.scalar.activation(W16[:, HI, q, 0:4, cols],
                                         bank[5][:, :].rearrange("p (k n) -> p k n", n=P), ACT.Copy)
                    nc.scalar.activation(W16[:, HI, q, 4:6, cols],
                                         bank[6][:, 0:2 * P].rearrange("p (k n) -> p k n", n=P),
                                         ACT.Copy).then_inc(w_hi, 1)
                if it == 6:
                    act.wait_ge(var_ready, 1)
                    nc.scalar.activation(sd[:, :], tmp[:, :], ACT.Sqrt).then_inc(sd_ready, 1)
                c = it - 8
                if 0 <= c < CHUNKS - 1:
                    act.wait_ge(h0_ready, c + 1)
                    nc.scalar.activation(state_n[:, HI, 4 * c:4 * c + 4, :], xs[:, 4 * c:4 * c + 4, :], ACT.Copy,
                                         scale=STATE_SCALE).then_inc(h0_hi, 1)
                if 0 <= c < CHUNKS:
                    for f in range(FT):
                        act.wait_ge(x_turned, 2 * c + f + 1)
                        nc.scalar.activation(state_t[:, f, chunk_of(c)], bank[5 + f][:, :],
                                             ACT.Copy).then_inc(state_new, 1)
            for c in range(CHUNKS):
                act.wait_ge(deg_summed, 2 * c + 2)
                nc.scalar.activation(deg_in[:, chunk_of(c)], bank[(2, 3, 4, 5)[c]][:, :], ACT.Copy)
                nc.scalar.activation(deg_out[:, chunk_of(c)], bank[(6, 7, 0, 1)[c]][:, :],
                                     ACT.Copy).then_inc(deg_ready, 1)
            act.wait_ge(scales_ready, 1)

            with act.Fori(0, STEPS) as t:
                def split_state(c):
                    for f in range(FT):
                        act.wait_ge(state_new, t * (CHUNKS * FT) + FT * c + f + 1)
                        nc.scalar.activation(ss[:, HI, f, :], state_t[:, f, chunk_of(c)], ACT.Copy,
                                             scale=k_scale[:, 0:1]).then_inc(s_hi, 1)

                def split_uv(c, g):
                    act.wait_ge(uv_summed, t * (CHUNKS * UV) + UV * c + g + 1)
                    user = c - 1 if g == 0 else c
                    if user >= 1:
                        act.wait_ge(uv_used, t * CHUNKS + user)
                    nc.scalar.activation(uv[:, uv_slot(c, g), HI, :], bank[g][:, :], ACT.Copy,
                                         scale=u_scale[:, 0:1]).then_inc(uv_hi, 1)

                def split_nodes(n):
                    c, b0, b1 = TURNS[n]
                    for j, b in enumerate((b0, b1)):
                        act.wait_ge(turned, t * (2 * CHUNKS) + 2 * n + j + 1)
                        nc.scalar.activation(state_n[:, HI, 4 * c + 2 * j:4 * c + 2 * j + 2, :],
                                             bank[b][:, :].rearrange("p (t d) -> p t d", d=D), ACT.Copy,
                                             scale=STATE_SCALE).then_inc(node_hi, 1)

                def switch_on(c, n):
                    q, m, b = GROUPS[n]
                    u = FT * q + m
                    act.wait_ge(gate_biased, t * (CHUNKS * G) + G * c + n + 1)
                    dst = zt[:, m, :] if q == Z else bank[b][:, :]
                    nc.scalar.activation(dst, bank[b][:, :], ACT.Tanh if q == H else ACT.Sigmoid,
                                         bias=gate_b[:, u:u + 1], scale=inv[:, u:u + 1]).then_inc(gate_on, 1)

                def split_rs(c):
                    act.wait_ge(gate_summed, t * (CHUNKS * G) + G * c + 4)
                    for f in range(FT):
                        act.wait_ge(rs_ready, t * (CHUNKS * FT) + FT * c + f + 1)
                        nc.scalar.activation(ss[:, HI, f, :], bank[6 + f][:, :], ACT.Copy,
                                             scale=k_scale[:, 0:1]).then_inc(rs_hi, 1)

                split_state(0)
                split_nodes(0)
                for g in range(UV):
                    split_uv(0, g)
                for c in range(CHUNKS):
                    last = c == CHUNKS - 1
                    if not last:
                        split_uv(c + 1, 0)
                    for n in range(4):
                        switch_on(c, n)
                        if last and n < 3:
                            split_nodes(n + 1)
                    split_rs(c)
                    if not last:
                        split_uv(c + 1, 1)
                    switch_on(c, 4)
                    switch_on(c, 5)
                    if not last:
                        split_state(c + 1)
                        split_uv(c + 1, 2)
                        split_uv(c + 1, 3)

            for w in range(4):
                act.wait_ge(head_turned, w + 1)
                dst = head_t[:, w, :, :] if w < 3 else neigh_t
                nc.scalar.activation(dst, bank[w][:, :].rearrange("p (k d) -> p k d", k=FT),
                                     ACT.Copy).then_inc(head_ready, 1)
            act.wait_ge(wsum_summed, 1)
            nc.scalar.activation(wsum_all, bank[3][:, 0:D], ACT.Copy).then_inc(wsum_ready, 1)
            for c in range(CHUNKS):
                for g in range(FT):
                    act.wait_ge(th_summed, FT * c + g + 1)
                    nc.scalar.activation(th[:, g, chunk_of(c)], bank[4 + (FT * c + g) % 4][:, :], ACT.Tanh,
                                         bias=o1b[:, g:g + 1]).then_inc(th_ready, 1)
            for c in range(CHUNKS):
                act.wait_ge(var2_ready, c + 1)
                nc.scalar.activation(sd[:, 4 * c:4 * c + 4], tmp[:, 4 * c:4 * c + 4], ACT.Sqrt).then_inc(sd2_ready, 1)
                for f in range(FT):
                    act.wait_ge(h2_turned, FT * c + f + 1)
                    nc.scalar.activation(h2t[:, f, chunk_of(c)], bank[4 + (FT * c + f) % 4][:, :],
                                         ACT.Copy).then_inc(h2t_ready, 1)

        @block.vector
        def _(dve):
            chain = [0]

            def link(ins):
                chain[0] += 1
                ins.then_inc(dve_chain, 1)
                dve.wait_ge(dve_chain, chain[0])

            def inverse_sd(sl):
                link(nc.vector.reciprocal(rstd[:, sl], sd[:, sl]))
                link(nc.vector.tensor_tensor(sd[:, sl], rstd[:, sl], rstd[:, sl], ALU.mult))
                link(nc.vector.tensor_tensor(sd[:, sl], sd[:, sl], tmp[:, sl], ALU.mult))
                link(nc.vector.tensor_scalar(sd[:, sl], sd[:, sl], -0.5, 1.5, ALU.mult, ALU.add))
                link(nc.vector.tensor_tensor(rstd[:, sl], rstd[:, sl], sd[:, sl], ALU.mult))

            def power_of_two(dst, src, exponent):
                link(nc.vector.tensor_scalar(dst.bitcast(I32), src.bitcast(I32), EXP_MASK, None, ALU.bitwise_and))
                link(nc.vector.tensor_scalar(dst.bitcast(I32), dst.bitcast(I32), -1.0, (exponent + 254) * MANT,
                                             ALU.mult, ALU.add))

            dve.wait_ge(ident16_ready, 1)
            for it in range(TILES):
                u = it
                if u < UNITS:
                    if u >= 2:
                        dve.wait_ge(w_combined, u - 1)
                    dve.wait_ge(w_turned, u + 1)
                    nc.vector.tensor_copy(wt[:, u % 2, :, :],
                                          bank[2][:, :].rearrange("p (k n) -> p k n", k=4)).then_inc(wt_ready, 1)
                u = it - 1
                if 0 <= u < UNITS:
                    dve.wait_ge(cw_ready, u + 1)
                    link(nc.vector.tensor_reduce(rowmax[:, u:u + 1], wst[:, u, :], AX.X, ALU.max,
                                                 apply_absolute_value=True))
                    link(nc.vector.tensor_scalar(rowmax[:, u:u + 1], rowmax[:, u:u + 1], 2.0 ** -100, None, ALU.max))
                    power_of_two(sigma[:, u:u + 1], rowmax[:, u:u + 1], 14)
                    nc.vector.tensor_scalar(wst[:, u, :], wst[:, u, :], sigma[:, u:u + 1], None,
                                            ALU.mult).then_inc(w_scaled, 1)
                u = it - 2
                if 0 <= u < UNITS:
                    q, m = divmod(u, FT)
                    cols = slice(m * P, (m + 1) * P)
                    dve.wait_ge(w_hi, u + 1)
                    nc.vector.tensor_tensor(W16[:, LO, q, 0:4, cols],
                                            bank[5][:, :].rearrange("p (k n) -> p k n", n=P),
                                            W16[:, HI, q, 0:4, cols], ALU.subtract)
                    nc.vector.tensor_tensor(W16[:, LO, q, 4:6, cols],
                                            bank[6][:, 0:2 * P].rearrange("p (k n) -> p k n", n=P),
                                            W16[:, HI, q, 4:6, cols], ALU.subtract).then_inc(w_split, 1)
                c = it - 3
                if 0 <= c < CHUNKS:
                    dve.wait_ge(x_loaded[c], 16)
                    for j in range(4):
                        link(nc.vector.bn_stats(stats[:, j, :], xs[:, 4 * c + j, :]))
                    for j in range(4):
                        link(nc.vector.bn_aggr(mv[:, 4 * c + j, :], stats[:, j, :]))
                    if c == CHUNKS - 1:
                        nc.vector.tensor_scalar(tmp[:, :], mv[:, :, 1], EPS, None, ALU.add).then_inc(var_ready, 1)
                if it == 7:
                    dve.wait_ge(sd_ready, 1)
                    inverse_sd(slice(0, TILES))
                c = it - 7
                if 0 <= c < CHUNKS:
                    for j in range(4 * c, 4 * c + 4):
                        link(nc.vector.tensor_scalar(xs[:, j, :], xs[:, j, :], mv[:, j, 0:1], rstd[:, j:j + 1],
                                                     ALU.subtract, ALU.mult))
                    nc.vector.tensor_scalar(xs[:, 4 * c:4 * c + 4, :], xs[:, 4 * c:4 * c + 4, :], 0.0, None,
                                            ALU.max).then_inc(h0_ready, 1)
                c = it - 8
                if 0 <= c < CHUNKS - 1:
                    dve.wait_ge(h0_hi, c + 1)
                    nc.vector.scalar_tensor_tensor(state_n[:, LO, 4 * c:4 * c + 4, :], xs[:, 4 * c:4 * c + 4, :],
                                                   STATE_SCALE, state_n[:, HI, 4 * c:4 * c + 4, :],
                                                   ALU.mult, ALU.subtract).then_inc(node_split, 2)
                if it == 9:
                    dve.wait_ge(w_rows_turned, UNITS)
                for half in range(2):
                    dve.wait_ge(adj_turned, 2 * it + half + 1)
                    nc.vector.tensor_copy(AT16[:, it, 8 * half:8 * half + 8, :],
                                          bank[half][:, :].bitcast(F16).rearrange("p (k n) -> p k n", n=P)
                                          ).then_inc(adj_t_ready, 1)
                dve.wait_ge(adj_cast, it + 1)
                nc.vector.tensor_scalar(deg_in[:, it * P:(it + 1) * P], ident16[:, :], deg_col[:, it:it + 1], None,
                                        ALU.mult).then_inc(diag_ready, 1)
            dve.wait_ge(deg_ready, CHUNKS)
            nc.vector.tensor_reduce(dmax[:, 0:1], deg_in[:, :], AX.X, ALU.max)
            link(nc.vector.tensor_reduce(dmax[:, 1:2], deg_out[:, :], AX.X, ALU.max))
            link(nc.vector.tensor_scalar(dmax[:, 0:1], dmax[:, 0:1], dmax[:, 1:2], 1.0, ALU.max, ALU.max))
            power_of_two(k_scale[:, 0:1], dmax[:, 0:1], 10)
            link(nc.vector.tensor_scalar(u_scale[:, 0:1], k_scale[:, 0:1], 1.0 / STATE_SCALE, None, ALU.mult))
            link(nc.vector.tensor_scalar(sigma[:, :], sigma[:, :], k_scale[:, 0:1], None, ALU.mult))
            for s in range(2):
                link(nc.vector.tensor_tensor(c_gate[:, :, s], c_gate[:, :, s], sigma[:, :], ALU.mult))
            nc.vector.reciprocal(inv[:, :], sigma[:, :]).then_inc(scales_ready, 1)

            LINKS = CHUNKS * (G + 2 * FT)
            with dve.Fori(0, STEPS) as t:
                links = [0]

                def step_link(ins):
                    links[0] += 1
                    ins.then_inc(step_chain, 1)
                    dve.wait_ge(step_chain, t * LINKS + links[0])

                def split_state(c):
                    for f in range(FT):
                        dve.wait_ge(s_hi, t * (CHUNKS * FT) + FT * c + f + 1)
                        nc.vector.scalar_tensor_tensor(ss[:, LO, f, :], state_t[:, f, chunk_of(c)],
                                                       k_scale[:, 0:1], ss[:, HI, f, :],
                                                       ALU.mult, ALU.subtract).then_inc(s_split, 1)

                def split_uv(c, g):
                    dve.wait_ge(uv_hi, t * (CHUNKS * UV) + UV * c + g + 1)
                    slot = uv_slot(c, g)
                    nc.vector.scalar_tensor_tensor(uv[:, slot, LO, :], bank[g][:, :], u_scale[:, 0:1],
                                                   uv[:, slot, HI, :], ALU.mult, ALU.subtract).then_inc(uv_split, 1)

                def split_nodes(n):
                    c, b0, b1 = TURNS[n]
                    for j, b in enumerate((b0, b1)):
                        dve.wait_ge(node_hi, t * (2 * CHUNKS) + 2 * n + j + 1)
                        rows = slice(4 * c + 2 * j, 4 * c + 2 * j + 2)
                        nc.vector.scalar_tensor_tensor(state_n[:, LO, rows, :],
                                                       bank[b][:, :].rearrange("p (t d) -> p t d", d=D),
                                                       STATE_SCALE, state_n[:, HI, rows, :],
                                                       ALU.mult, ALU.subtract).then_inc(node_split, 1)

                def add_degrees(c, n):
                    q, m, b = GROUPS[n]
                    u = FT * q + m
                    dve.wait_ge(gate_summed, t * (CHUNKS * G) + G * c + n + 1)
                    step_link(nc.vector.scalar_tensor_tensor(bank[b][:, :], deg_in[:, chunk_of(c)],
                                                             c_gate[:, u, 0:1], bank[b][:, :], ALU.mult, ALU.add))
                    nc.vector.scalar_tensor_tensor(bank[b][:, :], deg_out[:, chunk_of(c)], c_gate[:, u, 1:2],
                                                   bank[b][:, :], ALU.mult, ALU.add).then_inc(gate_biased, 1)

                def reset_state(c, f):
                    dve.wait_ge(gate_on, t * (CHUNKS * G) + G * c + 2 + f + 1)
                    nc.vector.tensor_tensor(bank[6 + f][:, :], bank[6 + f][:, :], state_t[:, f, chunk_of(c)],
                                            ALU.mult).then_inc(rs_ready, 1)

                def split_rs(c):
                    for f in range(FT):
                        dve.wait_ge(rs_hi, t * (CHUNKS * FT) + FT * c + f + 1)
                        nc.vector.scalar_tensor_tensor(ss[:, LO, f, :], bank[6 + f][:, :], k_scale[:, 0:1],
                                                       ss[:, HI, f, :], ALU.mult, ALU.subtract).then_inc(rs_split, 1)

                def update(c, f):
                    dve.wait_ge(gate_on, t * (CHUNKS * G) + G * c + 4 + f + 1)
                    h = bank[4 + f][:, :]
                    st = state_t[:, f, chunk_of(c)]
                    step_link(nc.vector.tensor_tensor(h, h, st, ALU.subtract))
                    step_link(nc.vector.tensor_tensor(h, h, zt[:, f, :], ALU.mult))
                    nc.vector.tensor_tensor(st, h, st, ALU.add).then_inc(state_new, 1)

                split_state(0)
                split_nodes(0)
                for g in range(UV):
                    split_uv(0, g)
                for c in range(CHUNKS):
                    last = c == CHUNKS - 1
                    if not last:
                        split_uv(c + 1, 0)
                    for n in range(4):
                        add_degrees(c, n)
                        if n >= 2:
                            reset_state(c, n - 2)
                        if last and n < 3:
                            split_nodes(n + 1)
                    split_rs(c)
                    if not last:
                        split_uv(c + 1, 1)
                    add_degrees(c, 4)
                    add_degrees(c, 5)
                    update(c, 0)
                    update(c, 1)
                    if not last:
                        split_state(c + 1)
                        split_uv(c + 1, 2)
                        split_uv(c + 1, 3)

            dve.wait_ge(head_loaded, 16 * 5)
            for c in range(CHUNKS):
                for j in range(2):
                    dve.wait_ge(xb_ready, 4 * c + 2 * j + 2)
                    dve.wait_ge(o2_summed, 2 * c + j + 1)
                    rows = slice(4 * c + 2 * j, 4 * c + 2 * j + 2)
                    link(nc.vector.tensor_tensor(x1[:, rows, :],
                                                 bank[(2 * c + j) % 4][:, :].rearrange("p (t d) -> p t d", d=D),
                                                 xr[:, rows, :], ALU.add))
                    nc.vector.engine_nop().then_inc(o2_taken, 1)
                for j in range(4):
                    link(nc.vector.bn_stats(stats[:, j, :], x1[:, 4 * c + j, :]))
                for j in range(4):
                    link(nc.vector.bn_aggr(mv[:, 4 * c + j, :], stats[:, j, :]))
                sl = slice(4 * c, 4 * c + 4)
                nc.vector.tensor_scalar(tmp[:, sl], mv[:, sl, 1], EPS, None, ALU.add).then_inc(var2_ready, 1)
                dve.wait_ge(sd2_ready, c + 1)
                inverse_sd(sl)
                for j in range(4 * c, 4 * c + 4):
                    link(nc.vector.tensor_scalar(h2[:, j, :], x1[:, j, :], mv[:, j, 0:1], rstd[:, j:j + 1],
                                                 ALU.subtract, ALU.mult))
                nc.vector.tensor_scalar(h2[:, sl, :], h2[:, sl, :], 0.0, None, ALU.max).then_inc(h2_ready, 1)
            dve.wait_ge(h2_ready, CHUNKS)
            link(nc.vector.tensor_scalar(h2col[:, :, 0], h2[:, :, 0], STATE_SCALE, None, ALU.mult))
            nc.vector.scalar_tensor_tensor(h2col[:, :, 1], h2[:, :, 0], STATE_SCALE, h2col[:, :, 0],
                                           ALU.mult, ALU.subtract).then_inc(h2col_ready, 1)
            dve.wait_ge(s_summed, 1)
            link(nc.vector.tensor_reduce(s_col[:, :], bank[0][:, 0:2 * TILES].rearrange("p (t s) -> p t s", s=2),
                                         AX.X, ALU.add))
            link(nc.vector.tensor_scalar(deg_col[:, :], deg_col[:, :], 0.0, 1.0 / STATE_SCALE, ALU.is_gt, ALU.mult))
            link(nc.vector.tensor_tensor(s_col[:, :], s_col[:, :], deg_col[:, :], ALU.mult))
            dve.wait_ge(wsum_ready, 1)
            for n in range(TILES):
                dve.wait_ge(self_summed, n // 2 + 1)
                src = bank[1 + (n // 2) % 3][:, (n % 2) * D:(n % 2 + 1) * D]
                link(nc.vector.scalar_tensor_tensor(h2[:, n, :], wsum_all, s_col[:, n:n + 1], src,
                                                    ALU.mult, ALU.add))
                if n % 2:
                    nc.vector.engine_nop().then_inc(self_taken, 1)
                nc.vector.scalar_tensor_tensor(x1[:, n, :], h2[:, n, :], 0.0, x1[:, n, :],
                                               ALU.max, ALU.add).then_inc(out_ready, 1)

        @block.tensor
        def _(pe):
            mm = nc.tensor.matmul
            pe.wait_ge(ident16_ready, 1)
            pe.wait_ge(weights_loaded, 16 * N_WEIGHT_DMAS)
            for it in range(TILES):
                u = it
                if u < UNITS:
                    if u >= 1:
                        pe.wait_ge(wt_ready, u)
                    for k in range(4):
                        last = nc.tensor.transpose(bank[2][:, k * P:(k + 1) * P], wst[:, u, k * P:(k + 1) * P],
                                                   ident[:, :])
                    last.then_inc(w_turned, 1)
                u = it - 1
                if 0 <= u < UNITS:
                    pe.wait_ge(wt_ready, u + 1)
                    if u >= 1:
                        pe.wait_ge(cw_ready, u)
                    for s in range(2):
                        for k in range(FT):
                            last = mm(bank[3 + s][:, 0:DB], wt[:, u % 2, FT * s + k, :], inw[:, s, k, :],
                                      start=(k == 0), stop=(k == FT - 1))
                    last.then_inc(w_combined, 1)
                u = it - 2
                if 0 <= u < UNITS:
                    pe.wait_ge(w_scaled, u + 1)
                    if u >= 1:
                        pe.wait_ge(w_split, u)
                    for k in range(KT):
                        last = nc.tensor.transpose(bank[5 + k // 4][:, (k % 4) * P:(k % 4 + 1) * P],
                                                   wst[:, u, k * P:(k + 1) * P], ident[:, :])
                    last.then_inc(w_rows_turned, 1)
                c = it - 8
                if 0 <= c < CHUNKS:
                    pe.wait_ge(h0_ready, c + 1)
                    if c == 0:
                        pe.wait_ge(w_split, UNITS)
                    else:
                        pe.wait_ge(state_new, FT * c)
                    for f in range(FT):
                        for j in range(4):
                            last = nc.tensor.transpose(bank[5 + f][:, j * P:(j + 1) * P],
                                                       xs[:, 4 * c + j, f * P:(f + 1) * P], ident[:, :])
                        last.then_inc(x_turned, 1)
                pe.wait_ge(adj_cast, it + 1)
                for half in range(2):
                    if it >= 1:
                        pe.wait_ge(adj_t_ready, 2 * it + half - 1)
                    for k in range(8):
                        jt = 8 * half + k
                        last = nc.tensor.transpose(bank[half][:, :].bitcast(F16)[:, k * P:(k + 1) * P],
                                                   A16[:, it, jt * P:(jt + 1) * P], ident16[:, :])
                    last.then_inc(adj_turned, 1)
            pe.wait_ge(diag_ready, TILES)
            pe.wait_ge(deg_added, TILES)
            pe.wait_ge(adj_t_ready, 2 * TILES)
            pe.wait_ge(state_new, FT * CHUNKS)
            pe.wait_ge(node_split, 2 * (CHUNKS - 1))
            for c in range(CHUNKS):
                mm(bank[(2, 3, 4, 5)[c]][:, :], ones16[:, :], deg_in[:, chunk_of(c)],
                   start=True, stop=True).then_inc(deg_summed, 1)
                mm(bank[(6, 7, 0, 1)[c]][:, :], ones16[:, :], deg_out[:, chunk_of(c)],
                   start=True, stop=True).then_inc(deg_summed, 1)
            pe.wait_ge(deg_ready, CHUNKS)

            with pe.Fori(0, STEPS) as t:
                def sum_group(c, g, tiles):
                    f = g % FT
                    for jt in tiles:
                        for part in (HI, LO):
                            last = mm(bank[g][:, :], state_n[:, part, jt, f * P:(f + 1) * P], adj_moving(g, jt, c),
                                      start=(jt == 0 and part == HI), stop=(jt == TILES - 1 and part == LO))
                    if tiles[-1] == TILES - 1:
                        last.then_inc(uv_summed, 1)

                def whole_group(c, g):
                    pe.wait_ge(uv_split, t * (CHUNKS * UV) + UV * (c - 1) + g + 1)
                    sum_group(c, g, range(TILES))

                def gate_terms(c, n, kts, first, final):
                    q, m, b = GROUPS[n]
                    for i, k in enumerate(kts):
                        if n == 0 and k < UV:
                            pe.wait_ge(uv_split, t * (CHUNKS * UV) + UV * c + k + 1)
                        for j, (wp, xp) in enumerate(((HI, HI), (LO, HI), (HI, LO))):
                            src = uv[:, uv_slot(c, k), xp, :] if k < UV else ss[:, xp, k - UV, :]
                            last = mm(bank[b][:, :], W16[:, wp, q, k, m * P:(m + 1) * P], src,
                                      start=(first and i == 0 and j == 0),
                                      stop=(final and i == len(kts) - 1 and j == 2))
                    return last

                def gates_rz(c, n):
                    if n < 2:
                        pe.wait_ge(state_new, (t + 1) * (CHUNKS * FT) + FT * c + n - 1)
                    if n == 0:
                        pe.wait_ge(s_split, t * (CHUNKS * FT) + FT * (c + 1))
                    gate_terms(c, n, (4, 5, 0, 1, 2, 3), True, True).then_inc(gate_summed, 1)

                def gates_h_uv(c):
                    for n in (4, 5):
                        pe.wait_ge(gate_on, t * (CHUNKS * G) + G * c + n - 3)
                        last = gate_terms(c, n, (0, 1, 2, 3), True, False)
                    last.then_inc(uv_used, 1)

                def gates_h_rs(c):
                    for n in (4, 5):
                        for f in range(FT):
                            pe.wait_ge(rs_split, t * (CHUNKS * FT) + FT * c + f + 1)
                            last = gate_terms(c, n, (UV + f,), False, f == FT - 1)
                        last.then_inc(gate_summed, 1)

                def turn(n):
                    c, b0, b1 = TURNS[n]
                    for j, b in enumerate((b0, b1)):
                        for k in range(2):
                            for f in range(FT):
                                jt = 4 * c + 2 * j + k
                                last = nc.tensor.transpose(bank[b][:, k * D + f * P:k * D + (f + 1) * P],
                                                           state_t[:, f, jt * P:(jt + 1) * P], ident[:, :])
                        last.then_inc(turned, 1)

                pe.wait_ge(node_split, t * (2 * CHUNKS) + 2 * (CHUNKS - 1))
                for g in range(UV):
                    if g == UV - 1:
                        pe.wait_ge(state_new, (t + 1) * (CHUNKS * FT))
                        turn(0)
                    sum_group(0, g, range(0, TILES - 4))
                pe.wait_ge(node_split, (t + 1) * (2 * CHUNKS))
                for g in range(UV):
                    sum_group(0, g, range(TILES - 4, TILES))
                for c in range(CHUNKS):
                    last_chunk = c == CHUNKS - 1
                    if not last_chunk:
                        whole_group(c + 1, 0)
                    for n in range(4):
                        gates_rz(c, n)
                        if last_chunk and n < 3:
                            if n == 0:
                                pe.wait_ge(uv_split, t * (CHUNKS * UV) + UV * c + 2)
                            elif n == 1:
                                pe.wait_ge(uv_split, t * (CHUNKS * UV) + UV * c + 4)
                            else:
                                pe.wait_ge(node_split, (t + 1) * (2 * CHUNKS) + 2)
                            pe.wait_ge(state_new, (t + 1) * (CHUNKS * FT) + FT * (n + 1))
                            turn(n + 1)
                    gates_h_uv(c)
                    if not last_chunk:
                        whole_group(c + 1, 1)
                    gates_h_rs(c)
                    if not last_chunk:
                        whole_group(c + 1, 2)
                        whole_group(c + 1, 3)

            pe.wait_ge(node_split, (STEPS + 1) * 2 * CHUNKS - 2)
            pe.wait_ge(head_loaded, 16 * 5)
            pe.wait_ge(ones_ready, 1)
            for w in range(4):
                for k in range(FT):
                    for g in range(FT):
                        last = nc.tensor.transpose(bank[w][:, k * D + g * P:k * D + (g + 1) * P],
                                                   head_n[:, w, g, k * P:(k + 1) * P], ident[:, :])
                last.then_inc(head_turned, 1)
            pe.wait_ge(head_ready, 4)
            for k in range(FT):
                last = mm(bank[3][:, 0:D], ones32, neigh_t[:, k, :], start=(k == 0), stop=(k == FT - 1))
            last.then_inc(wsum_summed, 1)
            pe.wait_ge(state_new, (STEPS + 1) * CHUNKS * FT)
            pe.wait_ge(wsum_ready, 1)

            def first_layer_out(c):
                for j in range(2):
                    b = 2 * c + j
                    if b >= 4:
                        pe.wait_ge(o2_taken, b - 3)
                    for i in range(2):
                        n = 4 * c + 2 * j + i
                        for k in range(FT):
                            last = mm(bank[b % 4][:, i * D:(i + 1) * D], th[:, k, n * P:(n + 1) * P],
                                      head_t[:, 1, k, :], start=(k == 0), stop=(k == FT - 1))
                    last.then_inc(o2_summed, 1)

            for c in range(CHUNKS + 1):
                if c < CHUNKS:
                    for g in range(FT):
                        b = FT * c + g
                        if b >= 4:
                            pe.wait_ge(th_ready, b - 3)
                        for k in range(FT):
                            last = mm(bank[4 + b % 4][:, :], head_t[:, 0, k, g * P:(g + 1) * P],
                                      state_t[:, k, chunk_of(c)], start=(k == 0), stop=(k == FT - 1))
                        last.then_inc(th_summed, 1)
                if c >= 1:
                    pe.wait_ge(th_ready, FT * c)
                    first_layer_out(c - 1)
            pe.wait_ge(th_ready, FT * CHUNKS)
            for c in range(CHUNKS):
                pe.wait_ge(h2_ready, c + 1)
                for f in range(FT):
                    b = FT * c + f
                    if b >= 4:
                        pe.wait_ge(h2t_ready, b - 3)
                    for j in range(4):
                        last = nc.tensor.transpose(bank[4 + b % 4][:, j * P:(j + 1) * P],
                                                   h2[:, 4 * c + j, f * P:(f + 1) * P], ident[:, :])
                    last.then_inc(h2_turned, 1)
            pe.wait_ge(h2col_ready, 1)
            pe.wait_ge(o2_taken, 2 * CHUNKS)
            for it in range(TILES):
                for jt in range(TILES):
                    last = mm(bank[0][:, 2 * it:2 * it + 2], AT16[:, it, jt, :], h2col[:, jt, :],
                              start=(jt == 0), stop=(jt == TILES - 1))
            last.then_inc(s_summed, 1)
            pe.wait_ge(h2t_ready, FT * CHUNKS)
            for n in range(TILES):
                if n % 2 == 0 and n >= 6:
                    pe.wait_ge(self_taken, n // 2 - 2)
                b = 1 + (n // 2) % 3
                for k in range(FT):
                    last = mm(bank[b][:, (n % 2) * D:(n % 2 + 1) * D], h2t[:, k, n * P:(n + 1) * P],
                              head_t[:, 2, k, :], start=(k == 0), stop=(k == FT - 1))
                if n % 2:
                    last.then_inc(self_summed, 1)


_INS = ['x', 'adj', 'L0_gnn_in_W', 'L0_gnn_in_b', 'L0_gnn_out_W', 'L0_gnn_out_b', 'L0_gnn_r_W', 'L0_gnn_r_b',
        'L0_gnn_z_W', 'L0_gnn_z_b', 'L0_gnn_h_W', 'L0_gnn_h_b', 'L0_gnn_o1_W', 'L0_gnn_o1_b', 'L0_gnn_o2_W',
        'L0_gnn_o2_b', 'L1_gnn_w_self', 'L1_gnn_w_neigh']


def kernel(**inputs):
    import numpy as np
    import concourse.bacc as bacc
    from concourse.bass_utils import run_bass_kernel_spmd

    nc = bacc.Bacc("TRN2", target_bir_lowering=False, num_devices=1)
    arrays, args = {}, []
    for name in _INS:
        a = np.ascontiguousarray(inputs[name])
        arrays[name + "_dram"] = a
        args.append(nc.dram_tensor(name + "_dram", a.shape, mybir.dt.from_np(a.dtype), kind="ExternalInput").ap())
    out = nc.dram_tensor("out_dram", (N, D), F32, kind="ExternalOutput").ap()
    gnn_kernel(nc, *args, out)
    r = run_bass_kernel_spmd(nc, [arrays], core_ids=[0])
    return r.results[0]["out_dram"]
```

```python
from contextlib import ExitStack

import concourse.bass as bass
from concourse import mybir

ALU = mybir.AluOpType
ACT = mybir.ActivationFunctionType
AX = mybir.AxisListType
F32 = mybir.dt.float32
F16 = mybir.dt.float16
I32 = mybir.dt.int32

P = 128
N = 2048
D = 256
STEPS = 5
TILES = N // P
CHUNK = 512
CHUNKS = N // CHUNK
PER_CHUNK = CHUNK // P
FT = D // P
KT = 3 * FT
UNITS = 3 * FT
R, Z, H = 0, 1, 2
HI, LO = 0, 1
EPS = 1e-5
STATE_SCALE = 2.0 ** 11
EXP_MASK = 0x7F800000
MANT = 2.0 ** 23
RSQRT_GUESS = 0x5F3759DF


def gnn_kernel(nc, x, adj, in_W, in_b, out_W, out_b, r_W, r_b, z_W, z_b, h_W, h_b,
               o1_W, o1_b, o2_W, o2_b, w_self, w_neigh, out):
    ctx = ExitStack()
    with ctx:
        ctx.enter_context(nc.allow_non_contiguous_dma(reason="biases as columns, 256 numbers each"))

        def sb(name, shape, dt):
            return ctx.enter_context(nc.sbuf_tensor(name, shape, dt))

        def sem(name):
            return ctx.enter_context(nc.semaphore(name))

        A16 = sb("A16", [P, TILES, N], F16)
        AT16 = sb("AT16", [P, TILES, TILES, P], F16)
        state_n = sb("state_n", [P, 2, TILES, D], F16)
        state_t = sb("state_t", [P, FT, N], F32)
        W16 = sb("W16", [P, 2, 3, KT, D], F16)
        deg_in = sb("deg_in", [P, N], F16)
        deg_out = sb("deg_out", [P, N], F16)
        work = sb("work", [P, 18 * 512], F16)
        ident = sb("ident", [P, P], F32)
        ident16 = sb("ident16", [P, P], F16)
        ones16 = sb("ones16", [P, P], F16)
        rowmax = sb("rowmax", [P, UNITS], F32)
        sigma = sb("sigma", [P, UNITS], F32)
        c_gate = sb("c_gate", [P, UNITS, 2], F32)
        gate_b = sb("gate_b", [P, UNITS], F32)
        inv = sb("inv", [P, UNITS], F32)
        o1b = sb("o1b", [P, FT], F32)
        deg_col = sb("deg_col", [P, TILES], F32)
        stats = sb("stats", [P, PER_CHUNK, 6], F32)
        mv = sb("mv", [P, TILES, 2], F32)
        half_v = sb("half_v", [P, TILES], F32)
        rstd = sb("rstd", [P, TILES], F32)
        tmp = sb("tmp", [P, TILES], F32)
        dmax = sb("dmax", [P, 2 * CHUNKS], F32)
        dtop = sb("dtop", [P, 1], F32)
        k_scale = sb("k_scale", [P, 1], F32)
        u_scale = sb("u_scale", [P, 1], F32)
        h2col = sb("h2col", [P, TILES, 2], F16)
        s_col = sb("s_col", [P, TILES], F32)

        uv = work[:, 0:5 * 1024].rearrange("p (s h n) -> p s h n", s=5, h=2)
        ss = work[:, 5 * 1024:7 * 1024].rearrange("p (h f n) -> p h f n", h=2, f=FT)
        zt = work[:, 7 * 1024:9 * 1024].bitcast(F32).rearrange("p (f n) -> p f n", f=FT)
        a_in = work[:, 0:8 * 1024].bitcast(I32).rearrange("p (b n) -> p b n", b=2)
        xs = A16[:, TILES - 4:TILES, :].rearrange("p a n -> p (a n)").bitcast(F32).rearrange("p (t d) -> p t d", d=D)
        tail = AT16[:, 9:16, :, :].rearrange("p a b c -> p (a b c)").bitcast(F32)
        wst = tail[:, 0:UNITS * 3 * D].rearrange("p (u k) -> p u k", u=UNITS)
        o = UNITS * 3 * D
        DB = D + 1
        inw = tail[:, o:o + 2 * FT * DB].rearrange("p (s k n) -> p s k n", s=2, k=FT)
        o += 2 * FT * DB
        wt = tail[:, o:o + 2 * 4 * P].rearrange("p (b k n) -> p b k n", b=2, k=4)
        late = A16[:, :, :].rearrange("p a n -> p (a n)").bitcast(F32)
        xr = late[:, 0:4096].rearrange("p (t d) -> p t d", d=D)
        x1 = late[:, 4096:8192].rearrange("p (t d) -> p t d", d=D)
        h2 = late[:, 8192:12288].rearrange("p (t d) -> p t d", d=D)
        head_n = late[:, 12288:14336].rearrange("p (w g d) -> p w g d", w=4, g=FT)
        head_t = late[:, 14336:15872].rearrange("p (w k d) -> p w k d", w=3, k=FT)
        o2b_all = late[:, 15872:16128]
        wsum_all = late[:, 16128:16384]
        neigh_t = work[:, 0:1024].bitcast(F32).rearrange("p (k d) -> p k d", k=FT)
        ones32 = work[:, 1024:1280].bitcast(F32)
        th = state_n[:, :, :, :].rearrange("p h t d -> p (h t d)").bitcast(F32).rearrange("p (g n) -> p g n", g=FT)
        h2t = state_t

        bank = [ctx.enter_context(nc.psum_tensor(f"bank{i}", [P, CHUNK], F32)) for i in range(8)]

        x_loaded = [sem(f"x_loaded{c}") for c in range(CHUNKS)]
        weights_loaded = sem("weights_loaded")
        adj_loaded = [sem(f"adj_loaded{b}") for b in range(2)]
        ident_zeroed = sem("ident_zeroed")
        ident_ready = sem("ident_ready")
        ident16_ready = sem("ident16_ready")
        adj_cast = sem("adj_cast")
        deg_added = sem("deg_added")
        adj_turned = sem("adj_turned")
        adj_t_ready = sem("adj_t_ready")
        w_turned = sem("w_turned")
        biases_loaded = sem("biases_loaded")
        wt_ready = sem("wt_ready")
        w_combined = sem("w_combined")
        cw_ready = sem("cw_ready")
        w_sigma = sem("w_sigma")
        w_scaled = sem("w_scaled")
        w_rows_turned = sem("w_rows_turned")
        w_hi = sem("w_hi")
        w_split = sem("w_split")
        dve_chain = sem("dve_chain")
        h0_signed = sem("h0_signed")
        h0_ready = sem("h0_ready")
        h0_hi = sem("h0_hi")
        x_turned = sem("x_turned")
        diag_ready = sem("diag_ready")
        deg_summed = sem("deg_summed")
        deg_maxed = sem("deg_maxed")
        deg_ready = sem("deg_ready")
        deg_half_added = sem("deg_half_added")
        scales_ready = sem("scales_ready")

        uv_summed = sem("uv_summed")
        uv_hi = sem("uv_hi")
        uv_split = sem("uv_split")
        uv_used = sem("uv_used")
        s_hi = sem("s_hi")
        s_split = sem("s_split")
        gate_summed = sem("gate_summed")
        gate_biased = sem("gate_biased")
        gate_on = sem("gate_on")
        rs_ready = sem("rs_ready")
        rs_hi = sem("rs_hi")
        rs_split = sem("rs_split")
        state_new = sem("state_new")
        turned = sem("turned")
        node_hi = sem("node_hi")
        node_split = sem("node_split")
        step_chain = sem("step_chain")

        xr_loaded = sem("xr_loaded")
        head_loaded = sem("head_loaded")
        ones_ready = sem("ones_ready")
        xb_ready = sem("xb_ready")
        head_turned = sem("head_turned")
        head_ready = sem("head_ready")
        wsum_summed = sem("wsum_summed")
        wsum_ready = sem("wsum_ready")
        th_summed = sem("th_summed")
        th_ready = sem("th_ready")
        o2_summed = sem("o2_summed")
        o2_taken = sem("o2_taken")
        h2_ready = sem("h2_ready")
        h2_turned = sem("h2_turned")
        h2t_ready = sem("h2t_ready")
        h2col_ready = sem("h2col_ready")
        s_summed = sem("s_summed")
        s_ready = sem("s_ready")
        self_summed = sem("self_summed")
        self_parked = sem("self_parked")
        out_ready = sem("out_ready")
        stored = sem("stored")

        N_WEIGHT_DMAS = 3 + 2 + 2
        DEG_SPLIT = 1152

        def chunk_of(c):
            return slice(c * CHUNK, (c + 1) * CHUNK)

        def adj_moving(g, jt, c):
            if g < FT:
                return AT16[:, PER_CHUNK * c:PER_CHUNK * (c + 1), jt, :]
            return A16[:, jt, chunk_of(c)]

        def uv_slot(c, g):
            return c % 2 if g == 0 else g + 1

        GROUPS = [(Z, 0, 4), (Z, 1, 5), (R, 0, 6), (R, 1, 7), (H, 0, 4), (H, 1, 5)]
        G = len(GROUPS)
        UV = 2 * FT
        TH_BANKS = [(6, 7), (4, 5)]
        TURNS = [(0, 1), (2, 3), (0, 1), (6, 7)]
        DEG_BANKS = [7, 7, 7, 7, 4, 5, 6, 7]

        block = ctx.enter_context(nc.Block())

        @block.sync
        def _(sp):
            for c in range(CHUNKS):
                sp.dma_start(xs[:, 4 * c:4 * c + 4, :],
                             x[chunk_of(c), :].rearrange("(t p) d -> p t d", p=P)).then_inc(x_loaded[c], 16)
            for q, src in enumerate((r_W, z_W, h_W)):
                sp.dma_start(wst[:, 2 * q:2 * q + 2, :],
                             src.rearrange("(m p) k -> p m k", p=P)).then_inc(weights_loaded, 16)
            for s, (src, b) in enumerate(((in_W, in_b), (out_W, out_b))):
                sp.dma_start(inw[:, s, :, 0:D], src.rearrange("(k p) d -> p k d", p=P)).then_inc(weights_loaded, 16)
                sp.dma_start(inw[:, s, :, D:DB],
                             b.rearrange("(k p a) -> p k a", p=P, a=1)).then_inc(weights_loaded, 16)
            for it in range(TILES):
                if it >= 2:
                    sp.wait_ge(adj_cast, it - 1)
                sp.dma_start(a_in[:, it % 2, :], adj[it * P:(it + 1) * P, :]).then_inc(adj_loaded[it % 2], 16)
                if it == 1:
                    for q, src in enumerate((r_b, z_b, h_b)):
                        sp.dma_start(gate_b[:, 2 * q:2 * q + 2],
                                     src.rearrange("(m p) -> p m", p=P)).then_inc(biases_loaded, 16)
                    sp.dma_start(o1b[:, :], o1_b.rearrange("(m p) -> p m", p=P)).then_inc(biases_loaded, 16)
            sp.wait_ge(uv_summed, STEPS * CHUNKS * UV)
            for w, src in enumerate((o1_W, o2_W, w_self, w_neigh)):
                sp.dma_start(head_n[:, w, :, :], src.rearrange("(g p) d -> p g d", p=P)).then_inc(head_loaded, 16)
            sp.dma_start(o2b_all, o2_b.rearrange("(a d) -> a d", a=1).broadcast_to([P, D])).then_inc(head_loaded, 16)
            for c in range(CHUNKS):
                sp.dma_start(xr[:, 4 * c:4 * c + 4, :],
                             x[chunk_of(c), :].rearrange("(t p) d -> p t d", p=P)).then_inc(xr_loaded, 16)
            for c in range(CHUNKS):
                sp.wait_ge(out_ready, 4 * (c + 1))
                sp.dma_start(out[chunk_of(c), :].rearrange("(t p) d -> p t d", p=P),
                             x1[:, 4 * c:4 * c + 4, :]).then_inc(stored, 16)
            sp.wait_ge(stored, 16 * CHUNKS)

        @block.gpsimd
        def _(pool):
            nc.gpsimd.memset(ident[:, :], 0.0).then_inc(ident_zeroed, 1)
            nc.gpsimd.memset(ones16[:, :], 1.0)
            pool.wait_ge(ident_zeroed, 1)
            nc.gpsimd.affine_select(out=ident[:, :], in_=ident[:, :], compare_op=ALU.not_equal, fill=1.0,
                                    base=0, pattern=[[-1, P]], channel_multiplier=1).then_inc(ident_ready, 1)
            pool.wait_ge(ident_ready, 1)
            nc.gpsimd.tensor_copy(ident16[:, :], ident[:, :]).then_inc(ident16_ready, 1)
            for it in range(TILES):
                if it < CHUNKS:
                    pool.wait_ge(h0_signed, it + 1)
                    rows = slice(4 * it, 4 * it + 4)
                    nc.gpsimd.tensor_scalar(xs[:, rows, :], xs[:, rows, :], 0.0, None, ALU.max).then_inc(h0_ready, 1)
                u = it - 1
                if 0 <= u < UNITS:
                    pool.wait_ge(w_sigma, u + 1)
                    nc.gpsimd.tensor_scalar(wst[:, u, :], wst[:, u, :], sigma[:, u:u + 1], None,
                                            ALU.mult).then_inc(w_scaled, 1)
                pool.wait_ge(adj_cast, it + 1)
                left = slice(0, DEG_SPLIT)
                if it == 0:
                    nc.gpsimd.tensor_copy(deg_out[:, left], A16[:, 0, left]).then_inc(deg_added, 1)
                else:
                    pool.wait_ge(deg_added, it)
                    nc.gpsimd.tensor_tensor(deg_out[:, left], deg_out[:, left], A16[:, it, left],
                                            ALU.add).then_inc(deg_added, 1)
            pool.wait_ge(uv_summed, STEPS * CHUNKS * UV)
            pool.wait_ge(uv_used, STEPS * CHUNKS)
            nc.gpsimd.memset(ones32, 1.0).then_inc(ones_ready, 1)
            pool.wait_ge(head_loaded, 16 * 5)
            pool.wait_ge(xr_loaded, 16 * CHUNKS)
            for t in range(TILES):
                nc.gpsimd.tensor_tensor(xr[:, t, :], xr[:, t, :], o2b_all, ALU.add).then_inc(xb_ready, 1)

        @block.scalar
        def _(act):
            for it in range(TILES):
                act.wait_ge(adj_loaded[it % 2], 16 * (it // 2 + 1))
                if it == TILES - 4:
                    act.wait_ge(x_turned, 2 * CHUNKS)
                    act.wait_ge(node_split, 2 * CHUNKS)
                nc.scalar.activation(A16[:, it, :], a_in[:, it % 2, :], ACT.Copy,
                                     accum_out=deg_col[:, it:it + 1]).then_inc(adj_cast, 1)
                u = it
                if u < UNITS:
                    if u >= 2:
                        act.wait_ge(w_combined, u - 1)
                    act.wait_ge(w_turned, u + 1)
                    nc.scalar.activation(wt[:, u % 2, :, :], bank[0][:, :].rearrange("p (k n) -> p k n", k=4),
                                         ACT.Copy).then_inc(wt_ready, 1)
                u = it - 1
                if 0 <= u < UNITS:
                    act.wait_ge(w_combined, u + 1)
                    nc.scalar.activation(wst[:, u, 0:D], bank[1][:, 0:D], ACT.Copy)
                    nc.scalar.activation(wst[:, u, D:2 * D], bank[2][:, 0:D], ACT.Copy)
                    nc.scalar.activation(c_gate[:, u, 0:1], bank[1][:, D:DB], ACT.Copy)
                    nc.scalar.activation(c_gate[:, u, 1:2], bank[2][:, D:DB], ACT.Copy).then_inc(cw_ready, 1)
                c = it - 1
                if 0 <= c < CHUNKS:
                    act.wait_ge(h0_ready, c + 1)
                    nc.scalar.activation(state_n[:, HI, 4 * c:4 * c + 4, :], xs[:, 4 * c:4 * c + 4, :], ACT.Copy,
                                         scale=STATE_SCALE).then_inc(h0_hi, 1)
                    for f, b in enumerate((7, 0)):
                        act.wait_ge(x_turned, 2 * c + f + 1)
                        nc.scalar.activation(state_t[:, f, chunk_of(c)], bank[b][:, :],
                                             ACT.Copy).then_inc(state_new, 1)
                u = it - 2
                if 0 <= u < UNITS:
                    q, m = divmod(u, FT)
                    act.wait_ge(w_rows_turned, u + 1)
                    cols = slice(m * P, (m + 1) * P)
                    nc.scalar.activation(W16[:, HI, q, 0:4, cols],
                                         bank[3][:, :].rearrange("p (k n) -> p k n", n=P), ACT.Copy)
                    nc.scalar.activation(W16[:, HI, q, 4:6, cols],
                                         bank[6][:, 0:2 * P].rearrange("p (k n) -> p k n", n=P),
                                         ACT.Copy).then_inc(w_hi, 1)
                if it >= 5 and it % 4 == 1:
                    c = it // 4 - 1
                    act.wait_ge(deg_maxed, c + 1)
                    nc.scalar.activation(deg_in[:, chunk_of(c)], bank[DEG_BANKS[c]][:, :],
                                         ACT.Copy).then_inc(deg_ready, 1)
            for i in range(CHUNKS - 1, 2 * CHUNKS):
                act.wait_ge(deg_maxed, i + 1)
                dst = deg_in[:, chunk_of(i)] if i < CHUNKS else deg_out[:, chunk_of(i - CHUNKS)]
                nc.scalar.activation(dst, bank[DEG_BANKS[i]][:, :], ACT.Copy).then_inc(deg_ready, 1)
            act.wait_ge(scales_ready, 1)
            act.wait_ge(biases_loaded, 16 * 4)

            def split_state(t, c):
                for f in range(FT):
                    act.wait_ge(state_new, t * (CHUNKS * FT) + FT * c + f + 1)
                    nc.scalar.activation(ss[:, HI, f, :], state_t[:, f, chunk_of(c)], ACT.Copy,
                                         scale=k_scale[:, 0:1]).then_inc(s_hi, 1)

            def split_uv(t, c, g):
                act.wait_ge(uv_summed, t * (CHUNKS * UV) + UV * c + g + 1)
                user = c - 1 if g == 0 else c
                if user >= 1:
                    act.wait_ge(uv_used, t * CHUNKS + user)
                nc.scalar.activation(uv[:, uv_slot(c, g), HI, :], bank[g][:, :], ACT.Copy,
                                     scale=u_scale[:, 0:1]).then_inc(uv_hi, 1)

            def split_nodes(t, c):
                for j, b in enumerate(TURNS[c]):
                    act.wait_ge(turned, t * (2 * CHUNKS) + 2 * c + j + 1)
                    nc.scalar.activation(state_n[:, HI, 4 * c + 2 * j:4 * c + 2 * j + 2, :],
                                         bank[b][:, :].rearrange("p (t d) -> p t d", d=D), ACT.Copy,
                                         scale=STATE_SCALE).then_inc(node_hi, 1)

            def switch_on(t, c, n):
                q, m, b = GROUPS[n]
                u = FT * q + m
                act.wait_ge(gate_biased, t * (CHUNKS * G) + G * c + n + 1)
                dst = zt[:, m, :] if q == Z else bank[b][:, :]
                nc.scalar.activation(dst, bank[b][:, :], ACT.Tanh if q == H else ACT.Sigmoid,
                                     bias=gate_b[:, u:u + 1], scale=inv[:, u:u + 1]).then_inc(gate_on, 1)

            def split_rs(t, c):
                act.wait_ge(gate_summed, t * (CHUNKS * G) + G * c + 4)
                for f in range(FT):
                    act.wait_ge(rs_ready, t * (CHUNKS * FT) + FT * c + f + 1)
                    nc.scalar.activation(ss[:, HI, f, :], bank[6 + f][:, :], ACT.Copy,
                                         scale=k_scale[:, 0:1]).then_inc(rs_hi, 1)

            def turned_heads():
                for w in range(4):
                    act.wait_ge(head_turned, w + 1)
                    dst = head_t[:, w, :, :] if w < 3 else neigh_t
                    nc.scalar.activation(dst, bank[w][:, :].rearrange("p (k d) -> p k d", k=FT),
                                         ACT.Copy).then_inc(head_ready, 1)

            def step(t, final):
                for c in range(CHUNKS):
                    last = c == CHUNKS - 1
                    if not last:
                        split_uv(t, c + 1, 0)
                    for n in range(4):
                        switch_on(t, c, n)
                        if last and n < 3 and not final:
                            split_nodes(t, n)
                    split_rs(t, c)
                    if not last:
                        split_uv(t, c + 1, 1)
                    elif final:
                        turned_heads()
                    switch_on(t, c, 4)
                    switch_on(t, c, 5)
                    if not last:
                        split_state(t, c + 1)
                        split_uv(t, c + 1, 2)
                        split_uv(t, c + 1, 3)
                if not final:
                    split_state(t + 1, 0)
                    split_nodes(t, CHUNKS - 1)
                    for g in range(UV):
                        split_uv(t + 1, 0, g)

            for g in range(UV):
                split_uv(0, 0, g)
            split_state(0, 0)
            with act.Fori(0, STEPS - 1) as t:
                step(t, False)
            step(STEPS - 1, True)

            for c in range(CHUNKS):
                for g in range(FT):
                    act.wait_ge(th_summed, FT * c + g + 1)
                    nc.scalar.activation(th[:, g, chunk_of(c)], bank[TH_BANKS[c % 2][g]][:, :], ACT.Tanh,
                                         bias=o1b[:, g:g + 1]).then_inc(th_ready, 1)
                if c == 0:
                    act.wait_ge(wsum_summed, 1)
                    nc.scalar.activation(wsum_all, bank[3][:, 0:D], ACT.Copy).then_inc(wsum_ready, 1)
            for c in range(CHUNKS):
                for f in range(FT):
                    act.wait_ge(h2_turned, FT * c + f + 1)
                    nc.scalar.activation(h2t[:, f, chunk_of(c)], bank[4 + (FT * c + f) % 3][:, :],
                                         ACT.Copy).then_inc(h2t_ready, 1)
                act.wait_ge(h2col_ready, c + 1)
                for j in range(2):
                    b = 2 * c + j
                    act.wait_ge(self_summed, b + 1)
                    nc.scalar.activation(h2[:, 2 * b:2 * b + 2, :],
                                         bank[b % 4][:, :].rearrange("p (t d) -> p t d", d=D),
                                         ACT.Copy).then_inc(self_parked, 1)

        @block.vector
        def _(dve):
            chain = [0]

            def link(ins):
                chain[0] += 1
                ins.then_inc(dve_chain, 1)
                dve.wait_ge(dve_chain, chain[0])

            def inverse_root(sl):
                link(nc.vector.tensor_scalar(tmp[:, sl], mv[:, sl, 1], EPS, None, ALU.add))
                link(nc.vector.tensor_scalar(half_v[:, sl], tmp[:, sl], -0.5, None, ALU.mult))
                link(nc.vector.tensor_scalar(rstd[:, sl].bitcast(I32), tmp[:, sl].bitcast(I32), 1, None,
                                             ALU.logical_shift_right))
                link(nc.vector.tensor_scalar(rstd[:, sl].bitcast(I32), rstd[:, sl].bitcast(I32), -1.0,
                                             float(RSQRT_GUESS), ALU.mult, ALU.add))
                for _ in range(4):
                    link(nc.vector.tensor_tensor(tmp[:, sl], rstd[:, sl], rstd[:, sl], ALU.mult))
                    link(nc.vector.tensor_tensor(tmp[:, sl], tmp[:, sl], half_v[:, sl], ALU.mult))
                    link(nc.vector.scalar_tensor_tensor(rstd[:, sl], tmp[:, sl], 1.5, rstd[:, sl],
                                                        ALU.add, ALU.mult))

            def power_of_two(dst, src, exponent):
                link(nc.vector.tensor_scalar(dst.bitcast(I32), src.bitcast(I32), EXP_MASK, None, ALU.bitwise_and))
                link(nc.vector.tensor_scalar(dst.bitcast(I32), dst.bitcast(I32), -1.0, (exponent + 254) * MANT,
                                             ALU.mult, ALU.add))

            for c in range(CHUNKS):
                dve.wait_ge(x_loaded[c], 16)
                if c >= 1:
                    dve.wait_ge(dve_chain, chain[0])
                for j in range(4):
                    ins = nc.vector.bn_stats(stats[:, j, :], xs[:, 4 * c + j, :])
                link(ins)
                for j in range(4):
                    ins = nc.vector.bn_aggr(mv[:, 4 * c + j, :], stats[:, j, :])
                link(ins)
            inverse_root(slice(0, TILES))
            dve.wait_ge(ident16_ready, 1)
            for it in range(TILES):
                if it < CHUNKS:
                    for j in range(4 * it, 4 * it + 4):
                        ins = nc.vector.tensor_scalar(xs[:, j, :], xs[:, j, :], mv[:, j, 0:1], rstd[:, j:j + 1],
                                                      ALU.subtract, ALU.mult)
                    ins.then_inc(h0_signed, 1)
                u = it - 1
                if 0 <= u < UNITS:
                    dve.wait_ge(cw_ready, u + 1)
                    link(nc.vector.tensor_reduce(rowmax[:, u:u + 1], wst[:, u, :], AX.X, ALU.max,
                                                 apply_absolute_value=True))
                    link(nc.vector.tensor_scalar(rowmax[:, u:u + 1], rowmax[:, u:u + 1], 2.0 ** -100, None, ALU.max))
                    power_of_two(sigma[:, u:u + 1], rowmax[:, u:u + 1], 14)
                    nc.vector.engine_nop().then_inc(w_sigma, 1)
                c = it - 2
                if 0 <= c < CHUNKS:
                    dve.wait_ge(h0_hi, c + 1)
                    nc.vector.scalar_tensor_tensor(state_n[:, LO, 4 * c:4 * c + 4, :], xs[:, 4 * c:4 * c + 4, :],
                                                   STATE_SCALE, state_n[:, HI, 4 * c:4 * c + 4, :],
                                                   ALU.mult, ALU.subtract).then_inc(node_split, 2)
                u = it - 2
                if 0 <= u < UNITS:
                    q, m = divmod(u, FT)
                    cols = slice(m * P, (m + 1) * P)
                    dve.wait_ge(w_hi, u + 1)
                    nc.vector.tensor_tensor(W16[:, LO, q, 0:4, cols],
                                            bank[3][:, :].rearrange("p (k n) -> p k n", n=P),
                                            W16[:, HI, q, 0:4, cols], ALU.subtract)
                    nc.vector.tensor_tensor(W16[:, LO, q, 4:6, cols],
                                            bank[6][:, 0:2 * P].rearrange("p (k n) -> p k n", n=P),
                                            W16[:, HI, q, 4:6, cols], ALU.subtract).then_inc(w_split, 1)
                if it >= 5 and it % 4 == 1:
                    c = it // 4 - 1
                    dve.wait_ge(deg_summed, c + 1)
                    nc.vector.tensor_reduce(dmax[:, c:c + 1], bank[DEG_BANKS[c]][:, :], AX.X,
                                            ALU.max).then_inc(deg_maxed, 1)
                dve.wait_ge(adj_cast, it + 1)
                nc.vector.tensor_scalar(deg_in[:, it * P:(it + 1) * P], ident16[:, :], deg_col[:, it:it + 1], None,
                                        ALU.mult).then_inc(diag_ready, 1)
                right = slice(DEG_SPLIT, N)
                if it == 0:
                    nc.vector.tensor_copy(deg_out[:, right], A16[:, 0, right]).then_inc(deg_half_added, 1)
                else:
                    dve.wait_ge(deg_half_added, it)
                    nc.vector.tensor_tensor(deg_out[:, right], deg_out[:, right], A16[:, it, right],
                                            ALU.add).then_inc(deg_half_added, 1)
                if it == 9:
                    dve.wait_ge(w_rows_turned, UNITS)
                for half in range(2):
                    dve.wait_ge(adj_turned, 2 * it + half + 1)
                    nc.vector.tensor_copy(AT16[:, it, 8 * half:8 * half + 8, :],
                                          bank[4 + half][:, :].bitcast(F16).rearrange("p (k n) -> p k n", n=P)
                                          ).then_inc(adj_t_ready, 1)
            for i in range(CHUNKS - 1, 2 * CHUNKS):
                dve.wait_ge(deg_summed, i + 1)
                nc.vector.tensor_reduce(dmax[:, i:i + 1], bank[DEG_BANKS[i]][:, :], AX.X,
                                        ALU.max).then_inc(deg_maxed, 1)
            dve.wait_ge(deg_maxed, 2 * CHUNKS)
            link(nc.vector.tensor_reduce(dtop[:, :], dmax[:, :], AX.X, ALU.max))
            link(nc.vector.tensor_scalar(dtop[:, :], dtop[:, :], 1.0, None, ALU.max))
            power_of_two(k_scale[:, 0:1], dtop[:, 0:1], 10)
            link(nc.vector.tensor_scalar(u_scale[:, 0:1], k_scale[:, 0:1], 1.0 / STATE_SCALE, None, ALU.mult))
            link(nc.vector.tensor_scalar(sigma[:, :], sigma[:, :], k_scale[:, 0:1], None, ALU.mult))
            for s in range(2):
                link(nc.vector.tensor_tensor(c_gate[:, :, s], c_gate[:, :, s], sigma[:, :], ALU.mult))
            nc.vector.reciprocal(inv[:, :], sigma[:, :]).then_inc(scales_ready, 1)

            LINKS = CHUNKS * (G + 2 * FT)
            links = [0]

            def step_link(t, ins):
                links[0] += 1
                ins.then_inc(step_chain, 1)
                dve.wait_ge(step_chain, t * LINKS + links[0])

            def split_state(t, c):
                for f in range(FT):
                    dve.wait_ge(s_hi, t * (CHUNKS * FT) + FT * c + f + 1)
                    nc.vector.scalar_tensor_tensor(ss[:, LO, f, :], state_t[:, f, chunk_of(c)],
                                                   k_scale[:, 0:1], ss[:, HI, f, :],
                                                   ALU.mult, ALU.subtract).then_inc(s_split, 1)

            def split_uv(t, c, g):
                dve.wait_ge(uv_hi, t * (CHUNKS * UV) + UV * c + g + 1)
                slot = uv_slot(c, g)
                nc.vector.scalar_tensor_tensor(uv[:, slot, LO, :], bank[g][:, :], u_scale[:, 0:1],
                                               uv[:, slot, HI, :], ALU.mult, ALU.subtract).then_inc(uv_split, 1)

            def split_nodes(t, c):
                for j, b in enumerate(TURNS[c]):
                    dve.wait_ge(node_hi, t * (2 * CHUNKS) + 2 * c + j + 1)
                    rows = slice(4 * c + 2 * j, 4 * c + 2 * j + 2)
                    nc.vector.scalar_tensor_tensor(state_n[:, LO, rows, :],
                                                   bank[b][:, :].rearrange("p (t d) -> p t d", d=D),
                                                   STATE_SCALE, state_n[:, HI, rows, :],
                                                   ALU.mult, ALU.subtract).then_inc(node_split, 1)

            def add_degrees(t, c, n):
                q, m, b = GROUPS[n]
                u = FT * q + m
                dve.wait_ge(gate_summed, t * (CHUNKS * G) + G * c + n + 1)
                step_link(t, nc.vector.scalar_tensor_tensor(bank[b][:, :], deg_in[:, chunk_of(c)],
                                                            c_gate[:, u, 0:1], bank[b][:, :], ALU.mult, ALU.add))
                nc.vector.scalar_tensor_tensor(bank[b][:, :], deg_out[:, chunk_of(c)], c_gate[:, u, 1:2],
                                               bank[b][:, :], ALU.mult, ALU.add).then_inc(gate_biased, 1)

            def reset_state(t, c, f):
                dve.wait_ge(gate_on, t * (CHUNKS * G) + G * c + 2 + f + 1)
                nc.vector.tensor_tensor(bank[6 + f][:, :], bank[6 + f][:, :], state_t[:, f, chunk_of(c)],
                                        ALU.mult).then_inc(rs_ready, 1)

            def split_rs(t, c):
                for f in range(FT):
                    dve.wait_ge(rs_hi, t * (CHUNKS * FT) + FT * c + f + 1)
                    nc.vector.scalar_tensor_tensor(ss[:, LO, f, :], bank[6 + f][:, :], k_scale[:, 0:1],
                                                   ss[:, HI, f, :], ALU.mult, ALU.subtract).then_inc(rs_split, 1)

            def update(t, c, f):
                dve.wait_ge(gate_on, t * (CHUNKS * G) + G * c + 4 + f + 1)
                h = bank[4 + f][:, :]
                st = state_t[:, f, chunk_of(c)]
                step_link(t, nc.vector.tensor_tensor(h, h, st, ALU.subtract))
                step_link(t, nc.vector.tensor_tensor(h, h, zt[:, f, :], ALU.mult))
                nc.vector.tensor_tensor(st, h, st, ALU.add).then_inc(state_new, 1)

            def step(t, final):
                links[0] = 0
                for c in range(CHUNKS):
                    last = c == CHUNKS - 1
                    if not last:
                        split_uv(t, c + 1, 0)
                    for n in range(4):
                        add_degrees(t, c, n)
                        if n >= 2:
                            reset_state(t, c, n - 2)
                        if last and n < 3 and not final:
                            split_nodes(t, n)
                    split_rs(t, c)
                    if not last:
                        split_uv(t, c + 1, 1)
                    add_degrees(t, c, 4)
                    add_degrees(t, c, 5)
                    update(t, c, 0)
                    update(t, c, 1)
                    if not last:
                        split_state(t, c + 1)
                        split_uv(t, c + 1, 2)
                        split_uv(t, c + 1, 3)
                if not final:
                    split_state(t + 1, 0)
                    split_nodes(t, CHUNKS - 1)
                    for g in range(UV):
                        split_uv(t + 1, 0, g)

            for g in range(UV):
                split_uv(0, 0, g)
            split_state(0, 0)
            with dve.Fori(0, STEPS - 1) as t:
                step(t, False)
            step(STEPS - 1, True)

            dve.wait_ge(head_loaded, 16 * 5)
            for c in range(CHUNKS):
                for j in range(2):
                    dve.wait_ge(xb_ready, 4 * c + 2 * j + 2)
                    dve.wait_ge(o2_summed, 2 * c + j + 1)
                    rows = slice(4 * c + 2 * j, 4 * c + 2 * j + 2)
                    link(nc.vector.tensor_tensor(x1[:, rows, :],
                                                 bank[(2 * c + j) % 4][:, :].rearrange("p (t d) -> p t d", d=D),
                                                 xr[:, rows, :], ALU.add))
                    nc.vector.engine_nop().then_inc(o2_taken, 1)
                for j in range(4):
                    ins = nc.vector.bn_stats(stats[:, j, :], x1[:, 4 * c + j, :])
                link(ins)
                for j in range(4):
                    ins = nc.vector.bn_aggr(mv[:, 4 * c + j, :], stats[:, j, :])
                link(ins)
                sl = slice(4 * c, 4 * c + 4)
                inverse_root(sl)
                for j in range(4 * c, 4 * c + 4):
                    ins = nc.vector.tensor_scalar(h2[:, j, :], x1[:, j, :], mv[:, j, 0:1], rstd[:, j:j + 1],
                                                  ALU.subtract, ALU.mult)
                link(ins)
                nc.vector.tensor_scalar(h2[:, sl, :], h2[:, sl, :], 0.0, None, ALU.max).then_inc(h2_ready, 1)
                dve.wait_ge(h2_ready, c + 1)
                link(nc.vector.tensor_scalar(h2col[:, sl, 0], h2[:, sl, 0], STATE_SCALE, None, ALU.mult))
                nc.vector.scalar_tensor_tensor(h2col[:, sl, 1], h2[:, sl, 0], STATE_SCALE, h2col[:, sl, 0],
                                               ALU.mult, ALU.subtract).then_inc(h2col_ready, 1)
            dve.wait_ge(s_summed, 1)
            link(nc.vector.tensor_reduce(s_col[:, :], bank[7][:, 0:2 * TILES].rearrange("p (t s) -> p t s", s=2),
                                         AX.X, ALU.add))
            link(nc.vector.tensor_scalar(deg_col[:, :], deg_col[:, :], 0.0, 1.0 / STATE_SCALE, ALU.is_gt, ALU.mult))
            link(nc.vector.tensor_tensor(s_col[:, :], s_col[:, :], deg_col[:, :], ALU.mult))
            dve.wait_ge(wsum_ready, 1)
            for c in range(CHUNKS):
                dve.wait_ge(self_parked, 2 * (c + 1))
                for n in range(4 * c, 4 * c + 4):
                    ins = nc.vector.scalar_tensor_tensor(h2[:, n, :], wsum_all, s_col[:, n:n + 1], h2[:, n, :],
                                                         ALU.mult, ALU.add)
                link(ins)
                for n in range(4 * c, 4 * c + 4):
                    nc.vector.scalar_tensor_tensor(x1[:, n, :], h2[:, n, :], 0.0, x1[:, n, :],
                                                   ALU.max, ALU.add).then_inc(out_ready, 1)

        @block.tensor
        def _(pe):
            mm = nc.tensor.matmul

            def sum_group(c, g, tiles):
                f = g % FT
                for jt in tiles:
                    for part in (HI, LO):
                        last = mm(bank[g][:, :], state_n[:, part, jt, f * P:(f + 1) * P], adj_moving(g, jt, c),
                                  start=(jt == 0 and part == HI), stop=(jt == TILES - 1 and part == LO))
                if tiles[-1] == TILES - 1:
                    last.then_inc(uv_summed, 1)

            FIRST = {8: (0, 0, 8), 9: (0, 8, 16), 10: (1, 0, 8), 11: (1, 8, 16),
                     12: (2, 0, 8), 13: (3, 0, 8), 14: (2, 8, 13), 15: (3, 8, 13)}
            pe.wait_ge(ident16_ready, 1)
            pe.wait_ge(weights_loaded, 16 * N_WEIGHT_DMAS)
            for it in range(TILES):
                u = it
                if u < UNITS:
                    if u >= 1:
                        pe.wait_ge(wt_ready, u)
                    if u >= 2:
                        pe.wait_ge(state_new, FT * min(u - 1, CHUNKS))
                    for k in range(4):
                        last = nc.tensor.transpose(bank[0][:, k * P:(k + 1) * P], wst[:, u, k * P:(k + 1) * P],
                                                   ident[:, :])
                    last.then_inc(w_turned, 1)
                u = it - 1
                if 0 <= u < UNITS:
                    pe.wait_ge(wt_ready, u + 1)
                    if u >= 1:
                        pe.wait_ge(cw_ready, u)
                    for s in range(2):
                        for k in range(FT):
                            last = mm(bank[1 + s][:, 0:DB], wt[:, u % 2, FT * s + k, :], inw[:, s, k, :],
                                      start=(k == 0), stop=(k == FT - 1))
                    last.then_inc(w_combined, 1)
                c = it - 1
                if 0 <= c < CHUNKS:
                    pe.wait_ge(h0_ready, c + 1)
                    pe.wait_ge(wt_ready, it + 1)
                    if c >= 1:
                        pe.wait_ge(state_new, FT * c)
                    for f, b in enumerate((7, 0)):
                        for j in range(4):
                            last = nc.tensor.transpose(bank[b][:, j * P:(j + 1) * P],
                                                       xs[:, 4 * c + j, f * P:(f + 1) * P], ident[:, :])
                        last.then_inc(x_turned, 1)
                u = it - 2
                if 0 <= u < UNITS:
                    pe.wait_ge(w_scaled, u + 1)
                    if u >= 1:
                        pe.wait_ge(w_split, u)
                    for k in range(KT):
                        last = nc.tensor.transpose(bank[(3, 6)[k // 4]][:, (k % 4) * P:(k % 4 + 1) * P],
                                                   wst[:, u, k * P:(k + 1) * P], ident[:, :])
                    last.then_inc(w_rows_turned, 1)
                if it >= 5 and it % 4 == 1:
                    c = it // 4 - 1
                    pe.wait_ge(diag_ready, 4 * (c + 1))
                    if c == 0:
                        pe.wait_ge(state_new, FT * CHUNKS)
                    else:
                        pe.wait_ge(deg_ready, c)
                    mm(bank[DEG_BANKS[c]][:, :], ones16[:, :], deg_in[:, chunk_of(c)],
                       start=True, stop=True).then_inc(deg_summed, 1)
                pe.wait_ge(adj_cast, it + 1)
                for half in range(2):
                    if it >= 1:
                        pe.wait_ge(adj_t_ready, 2 * it + half - 1)
                    for k in range(8):
                        jt = 8 * half + k
                        last = nc.tensor.transpose(bank[4 + half][:, :].bitcast(F16)[:, k * P:(k + 1) * P],
                                                   A16[:, it, jt * P:(jt + 1) * P], ident16[:, :])
                    last.then_inc(adj_turned, 1)
                if it == 8:
                    pe.wait_ge(w_split, UNITS)
                    pe.wait_ge(node_split, 2 * CHUNKS)
                if it in FIRST:
                    g, a, b = FIRST[it]
                    sum_group(0, g, range(a, b))
            sum_group(0, 2, range(13, TILES))
            sum_group(0, 3, range(13, TILES))
            pe.wait_ge(diag_ready, TILES)
            pe.wait_ge(deg_added, TILES)
            pe.wait_ge(deg_half_added, TILES)
            pe.wait_ge(adj_t_ready, 2 * TILES)
            for i in range(CHUNKS - 1, 2 * CHUNKS):
                if i == CHUNKS - 1:
                    pe.wait_ge(deg_ready, CHUNKS - 1)
                elif DEG_BANKS[i] == 7:
                    pe.wait_ge(deg_ready, CHUNKS)
                src = deg_in[:, chunk_of(i)] if i < CHUNKS else deg_out[:, chunk_of(i - CHUNKS)]
                mm(bank[DEG_BANKS[i]][:, :], ones16[:, :], src, start=True, stop=True).then_inc(deg_summed, 1)
            pe.wait_ge(deg_ready, 2 * CHUNKS)

            def whole_group(t, c, g):
                pe.wait_ge(uv_split, t * (CHUNKS * UV) + UV * (c - 1) + g + 1)
                sum_group(c, g, range(TILES))

            def gate_terms(t, c, n, kts, first, final):
                q, m, b = GROUPS[n]
                for i, k in enumerate(kts):
                    if n == 0 and k < UV:
                        pe.wait_ge(uv_split, t * (CHUNKS * UV) + UV * c + k + 1)
                    for j, (wp, xp) in enumerate(((HI, HI), (LO, HI), (HI, LO))):
                        src = uv[:, uv_slot(c, k), xp, :] if k < UV else ss[:, xp, k - UV, :]
                        last = mm(bank[b][:, :], W16[:, wp, q, k, m * P:(m + 1) * P], src,
                                  start=(first and i == 0 and j == 0),
                                  stop=(final and i == len(kts) - 1 and j == 2))
                return last

            def gates_rz(t, c, n):
                if n < 2:
                    pe.wait_ge(state_new, (t + 1) * (CHUNKS * FT) + FT * c + n - 1)
                if n == 0:
                    pe.wait_ge(s_split, t * (CHUNKS * FT) + FT * (c + 1))
                gate_terms(t, c, n, (4, 5, 0, 1, 2, 3), True, True).then_inc(gate_summed, 1)

            def gates_h_uv(t, c):
                for n in (4, 5):
                    pe.wait_ge(gate_on, t * (CHUNKS * G) + G * c + n - 3)
                    last = gate_terms(t, c, n, (0, 1, 2, 3), True, False)
                last.then_inc(uv_used, 1)

            def gates_h_rs(t, c):
                for n in (4, 5):
                    for f in range(FT):
                        pe.wait_ge(rs_split, t * (CHUNKS * FT) + FT * c + f + 1)
                        last = gate_terms(t, c, n, (UV + f,), False, f == FT - 1)
                    last.then_inc(gate_summed, 1)

            def turn(t, c):
                pe.wait_ge(state_new, (t + 1) * (CHUNKS * FT) + FT * (c + 1))
                for j, b in enumerate(TURNS[c]):
                    for k in range(2):
                        for f in range(FT):
                            jt = 4 * c + 2 * j + k
                            last = nc.tensor.transpose(bank[b][:, k * D + f * P:k * D + (f + 1) * P],
                                                       state_t[:, f, jt * P:(jt + 1) * P], ident[:, :])
                    last.then_inc(turned, 1)

            def turn_heads():
                pe.wait_ge(uv_split, STEPS * CHUNKS * UV)
                pe.wait_ge(head_loaded, 16 * 5)
                for w in range(4):
                    for k in range(FT):
                        for g in range(FT):
                            last = nc.tensor.transpose(bank[w][:, k * D + g * P:k * D + (g + 1) * P],
                                                       head_n[:, w, g, k * P:(k + 1) * P], ident[:, :])
                    last.then_inc(head_turned, 1)

            def step(t, final):
                for c in range(CHUNKS):
                    last_chunk = c == CHUNKS - 1
                    if not last_chunk:
                        whole_group(t, c + 1, 0)
                    for n in range(4):
                        gates_rz(t, c, n)
                        if last_chunk and n < 3 and not final:
                            if n == 0:
                                pe.wait_ge(uv_split, t * (CHUNKS * UV) + UV * c + 2)
                            elif n == 1:
                                pe.wait_ge(uv_split, t * (CHUNKS * UV) + UV * c + 4)
                            else:
                                pe.wait_ge(node_split, (t + 1) * (2 * CHUNKS) + 2)
                            turn(t, n)
                    gates_h_uv(t, c)
                    if not last_chunk:
                        whole_group(t, c + 1, 1)
                    elif final:
                        turn_heads()
                    gates_h_rs(t, c)
                    if not last_chunk:
                        whole_group(t, c + 1, 2)
                        whole_group(t, c + 1, 3)
                if not final:
                    pe.wait_ge(node_split, (t + 1) * (2 * CHUNKS) + 2 * (CHUNKS - 1))
                    for g in range(UV):
                        if g == UV - 1:
                            turn(t, CHUNKS - 1)
                        sum_group(0, g, range(0, TILES - 4))
                    pe.wait_ge(node_split, (t + 2) * (2 * CHUNKS))
                    for g in range(UV):
                        sum_group(0, g, range(TILES - 4, TILES))

            with pe.Fori(0, STEPS - 1) as t:
                step(t, False)
            step(STEPS - 1, True)

            def first_layer_hidden(c):
                pe.wait_ge(head_ready, 4)
                pe.wait_ge(state_new, STEPS * CHUNKS * FT + FT * (CHUNKS if c == 1 else c + 1))
                if c >= 2:
                    pe.wait_ge(th_ready, FT * (c - 1))
                for g, b in enumerate(TH_BANKS[c % 2]):
                    for k in range(FT):
                        last = mm(bank[b][:, :], head_t[:, 0, k, g * P:(g + 1) * P],
                                  state_t[:, k, chunk_of(c)], start=(k == 0), stop=(k == FT - 1))
                    last.then_inc(th_summed, 1)

            def first_layer_out(c):
                pe.wait_ge(th_ready, FT * (c + 1))
                for j in range(2):
                    b = 2 * c + j
                    if b == 3:
                        pe.wait_ge(wsum_ready, 1)
                    if b >= 4:
                        pe.wait_ge(o2_taken, b - 3)
                    for i in range(2):
                        n = 2 * b + i
                        for k in range(FT):
                            last = mm(bank[b % 4][:, i * D:(i + 1) * D], th[:, k, n * P:(n + 1) * P],
                                      head_t[:, 1, k, :], start=(k == 0), stop=(k == FT - 1))
                    last.then_inc(o2_summed, 1)

            def turn_h2(c):
                pe.wait_ge(h2_ready, c + 1)
                for f in range(FT):
                    b = FT * c + f
                    if b >= 3:
                        pe.wait_ge(h2t_ready, b - 2)
                    for j in range(4):
                        last = nc.tensor.transpose(bank[4 + b % 3][:, j * P:(j + 1) * P],
                                                   h2[:, 4 * c + j, f * P:(f + 1) * P], ident[:, :])
                    last.then_inc(h2_turned, 1)

            def sum_neighbours(c):
                pe.wait_ge(h2col_ready, c + 1)
                for jt in range(4 * c, 4 * c + 4):
                    for it in range(TILES):
                        last = mm(bank[7][:, 2 * it:2 * it + 2], AT16[:, it, jt, :], h2col[:, jt, :],
                                  start=(jt == 0 and it == 0), stop=(jt == TILES - 1), skip_group_check=True)
                if c == CHUNKS - 1:
                    last.then_inc(s_summed, 1)

            def own_term(c):
                pe.wait_ge(h2t_ready, FT * (c + 1))
                for j in range(2):
                    b = 2 * c + j
                    pe.wait_ge(*((o2_taken, 2 * CHUNKS - 4 + b + 1) if b < 4 else (self_parked, b - 3)))
                    for i in range(2):
                        n = 2 * b + i
                        for k in range(FT):
                            last = mm(bank[b % 4][:, i * D:(i + 1) * D], h2t[:, k, n * P:(n + 1) * P],
                                      head_t[:, 2, k, :], start=(k == 0), stop=(k == FT - 1))
                    last.then_inc(self_summed, 1)

            first_layer_hidden(0)
            pe.wait_ge(ones_ready, 1)
            for k in range(FT):
                last = mm(bank[3][:, 0:D], ones32, neigh_t[:, k, :], start=(k == 0), stop=(k == FT - 1))
            last.then_inc(wsum_summed, 1)
            first_layer_hidden(1)
            first_layer_out(0)
            first_layer_hidden(2)
            first_layer_out(1)
            first_layer_hidden(3)
            first_layer_out(2)
            first_layer_out(3)
            pe.wait_ge(th_ready, FT * CHUNKS)
            turn_h2(0)
            for c in range(CHUNKS):
                sum_neighbours(c)
                if c < CHUNKS - 1:
                    own_term(c)
                    turn_h2(c + 1)
                else:
                    own_term(c)


_INS = ['x', 'adj', 'L0_gnn_in_W', 'L0_gnn_in_b', 'L0_gnn_out_W', 'L0_gnn_out_b', 'L0_gnn_r_W', 'L0_gnn_r_b',
        'L0_gnn_z_W', 'L0_gnn_z_b', 'L0_gnn_h_W', 'L0_gnn_h_b', 'L0_gnn_o1_W', 'L0_gnn_o1_b', 'L0_gnn_o2_W',
        'L0_gnn_o2_b', 'L1_gnn_w_self', 'L1_gnn_w_neigh']


def kernel(**inputs):
    import numpy as np
    import concourse.bacc as bacc
    from concourse.bass_utils import run_bass_kernel_spmd

    nc = bacc.Bacc("TRN2", target_bir_lowering=False, num_devices=1)
    arrays, args = {}, []
    for name in _INS:
        a = np.ascontiguousarray(inputs[name])
        arrays[name + "_dram"] = a
        args.append(nc.dram_tensor(name + "_dram", a.shape, mybir.dt.from_np(a.dtype), kind="ExternalInput").ap())
    out = nc.dram_tensor("out_dram", (N, D), F32, kind="ExternalOutput").ap()
    gnn_kernel(nc, *args, out)
    r = run_bass_kernel_spmd(nc, [arrays], core_ids=[0])
    return r.results[0]["out_dram"]
```

```python
from contextlib import ExitStack

import concourse.bass as bass
from concourse import mybir

ALU = mybir.AluOpType
ACT = mybir.ActivationFunctionType
AX = mybir.AxisListType
F32 = mybir.dt.float32
F16 = mybir.dt.float16
I32 = mybir.dt.int32

P = 128
N = 2048
D = 256
STEPS = 5
TILES = N // P
CHUNK = 512
CHUNKS = N // CHUNK
PER_CHUNK = CHUNK // P
FT = D // P
KT = 3 * FT
UNITS = 3 * FT
R, Z, H = 0, 1, 2
HI, LO = 0, 1
O1, SELF, O2, NEIGH = 0, 1, 2, 3
EPS = 1e-5
STATE_SCALE = 2.0 ** 11
EXP_MASK = 0x7F800000
MANT = 2.0 ** 23
RSQRT_GUESS = 0x5F3759DF


def gnn_kernel(nc, x, adj, in_W, in_b, out_W, out_b, r_W, r_b, z_W, z_b, h_W, h_b,
               o1_W, o1_b, o2_W, o2_b, w_self, w_neigh, out):
    ctx = ExitStack()
    with ctx:
        ctx.enter_context(nc.allow_non_contiguous_dma(reason="biases as columns, 256 numbers each"))

        def sb(name, shape, dt):
            return ctx.enter_context(nc.sbuf_tensor(name, shape, dt))

        def sem(name):
            return ctx.enter_context(nc.semaphore(name))

        A16 = sb("A16", [P, TILES, N], F16)
        AT16 = sb("AT16", [P, TILES, TILES, P], F16)
        state_n = sb("state_n", [P, 2, TILES, D], F16)
        state_t = sb("state_t", [P, FT, N], F32)
        W16 = sb("W16", [P, 2, 3, KT, D], F16)
        deg_in = sb("deg_in", [P, N], F16)
        deg_out = sb("deg_out", [P, N], F16)
        work = sb("work", [P, 18 * 512], F16)
        ident = sb("ident", [P, P], F32)
        ident16 = sb("ident16", [P, P], F16)
        ones16 = sb("ones16", [P, P], F16)
        rowmax = sb("rowmax", [P, UNITS], F32)
        sigma = sb("sigma", [P, UNITS], F32)
        c_gate = sb("c_gate", [P, UNITS, 2], F32)
        gate_b = sb("gate_b", [P, UNITS], F32)
        inv = sb("inv", [P, UNITS], F32)
        o1b = sb("o1b", [P, FT], F32)
        deg_col = sb("deg_col", [P, TILES], F32)
        stats = sb("stats", [P, PER_CHUNK, 6], F32)
        mv = sb("mv", [P, TILES, 2], F32)
        half_v = sb("half_v", [P, TILES], F32)
        rstd = sb("rstd", [P, TILES], F32)
        tmp = sb("tmp", [P, TILES], F32)
        dmax = sb("dmax", [P, 2 * CHUNKS], F32)
        dtop = sb("dtop", [P, 1], F32)
        k_scale = sb("k_scale", [P, 1], F32)
        u_scale = sb("u_scale", [P, 1], F32)
        h2col = sb("h2col", [P, TILES, 2], F16)
        s_col = sb("s_col", [P, TILES], F32)

        uv = work[:, 0:5 * 1024].rearrange("p (s h n) -> p s h n", s=5, h=2)
        ss = work[:, 5 * 1024:7 * 1024].rearrange("p (h f n) -> p h f n", h=2, f=FT)
        zt = work[:, 7 * 1024:9 * 1024].bitcast(F32).rearrange("p (f n) -> p f n", f=FT)
        a_in = work[:, 0:8 * 1024].bitcast(I32).rearrange("p (b n) -> p b n", b=2)
        xs = A16[:, TILES - 4:TILES, :].rearrange("p a n -> p (a n)").bitcast(F32).rearrange("p (t d) -> p t d", d=D)
        tail = AT16[:, 9:16, :, :].rearrange("p a b c -> p (a b c)").bitcast(F32)
        wst = tail[:, 0:UNITS * 3 * D].rearrange("p (u k) -> p u k", u=UNITS)
        o = UNITS * 3 * D
        DB = D + 1
        inw = tail[:, o:o + 2 * FT * DB].rearrange("p (s k n) -> p s k n", s=2, k=FT)
        o += 2 * FT * DB
        wt = tail[:, o:o + 2 * 4 * P].rearrange("p (b k n) -> p b k n", b=2, k=4)
        late = A16[:, :, :].rearrange("p a n -> p (a n)").bitcast(F32)
        xr = late[:, 0:4096].rearrange("p (t d) -> p t d", d=D)
        x1 = late[:, 4096:8192].rearrange("p (t d) -> p t d", d=D)
        h2 = late[:, 8192:12288].rearrange("p (t d) -> p t d", d=D)
        head_n = late[:, 12288:14336].rearrange("p (w g d) -> p w g d", w=4, g=FT)
        head_t = A16[:, :, :].rearrange("p a n -> p (a n)")[:, 2 * 14336:2 * 15360].rearrange(
            "p (h w k d) -> p h w k d", h=2, w=2, k=FT)
        o2_t = late[:, 15360:15872].rearrange("p (k d) -> p k d", k=FT)
        o2b_all = late[:, 15872:16128]
        wsum_all = late[:, 16128:16384]
        fin = A16[:, :, :].rearrange("p a n -> p (a n)")[:, 2 * 8192:2 * 12288].rearrange(
            "p (c h f n) -> p c h f n", c=CHUNKS, h=2, f=FT)
        neigh_t = work[:, 1024:2048].bitcast(F32).rearrange("p (k d) -> p k d", k=FT)
        ones32 = work[:, 0:256].bitcast(F32)
        th = state_n[:, :, :, :].rearrange("p h t d -> p (h t d)").bitcast(F32).rearrange("p (g n) -> p g n", g=FT)
        h2t = state_t[:, :, :].rearrange("p f n -> p (f n)").bitcast(F16).rearrange("p (h f n) -> p h f n", h=2, f=FT)
        head_max = rowmax[:, 0:2]
        head_scale = sigma[:, 0:2]
        head_inv = sigma[:, 3:5]
        shift = half_v

        psum = ctx.enter_context(nc.psum_tensor("psum", [P, 8, CHUNK], F32))
        bank = [psum[:, i, :] for i in range(8)]

        x_loaded = [sem(f"x_loaded{c}") for c in range(CHUNKS)]
        weights_loaded = sem("weights_loaded")
        adj_loaded = [sem(f"adj_loaded{b}") for b in range(2)]
        ident_zeroed = sem("ident_zeroed")
        ident_ready = sem("ident_ready")
        ident16_ready = sem("ident16_ready")
        adj_cast = sem("adj_cast")
        deg_added = sem("deg_added")
        adj_turned = sem("adj_turned")
        adj_t_ready = sem("adj_t_ready")
        w_turned = sem("w_turned")
        biases_loaded = sem("biases_loaded")
        wt_ready = sem("wt_ready")
        w_combined = sem("w_combined")
        cw_ready = sem("cw_ready")
        w_scaled = sem("w_scaled")
        w_rows_turned = sem("w_rows_turned")
        w_hi = sem("w_hi")
        w_split = sem("w_split")
        dve_chain = sem("dve_chain")
        h0_ready = sem("h0_ready")
        h0_hi = sem("h0_hi")
        h0_hi_own = sem("h0_hi_own")
        x_turned = sem("x_turned")
        diag_ready = sem("diag_ready")
        deg_summed = sem("deg_summed")
        deg_maxed = sem("deg_maxed")
        deg_ready = sem("deg_ready")
        deg_half_added = sem("deg_half_added")
        u_scale_ready = sem("u_scale_ready")
        scales_ready = sem("scales_ready")

        uv_summed = sem("uv_summed")
        uv_hi = sem("uv_hi")
        uv_split = sem("uv_split")
        uv_used = sem("uv_used")
        s_hi = sem("s_hi")
        s_split = sem("s_split")
        gate_summed = sem("gate_summed")
        gate_biased = sem("gate_biased")
        gate_on = sem("gate_on")
        rs_ready = sem("rs_ready")
        rs_hi = sem("rs_hi")
        rs_split = sem("rs_split")
        state_new = sem("state_new")
        turned = sem("turned")
        node_hi = sem("node_hi")
        node_split = sem("node_split")
        step_chain = sem("step_chain")

        xr_loaded = sem("xr_loaded")
        head_loaded = sem("head_loaded")
        ones_ready = sem("ones_ready")
        xb_ready = sem("xb_ready")
        head_maxed = sem("head_maxed")
        head_max_summed = sem("head_max_summed")
        head_scaled = sem("head_scaled")
        head_turned = sem("head_turned")
        head_hi = sem("head_hi")
        head_split = sem("head_split")
        neigh_ready = sem("neigh_ready")
        final_hi = sem("final_hi")
        final_split = sem("final_split")
        o2_ready = sem("o2_ready")
        norm_ready = sem("norm_ready")
        h2t_hi = sem("h2t_hi")
        h2t_split = sem("h2t_split")
        wsum_summed = sem("wsum_summed")
        wsum_ready = sem("wsum_ready")
        th_summed = sem("th_summed")
        th_ready = sem("th_ready")
        o2_summed = sem("o2_summed")
        o2_taken = sem("o2_taken")
        h2_ready = sem("h2_ready")
        h2_turned = sem("h2_turned")
        h2col_ready = sem("h2col_ready")
        s_summed = sem("s_summed")
        self_summed = sem("self_summed")
        self_parked = sem("self_parked")
        both_added = sem("both_added")
        out_ready = sem("out_ready")
        stored = sem("stored")

        N_WEIGHT_DMAS = 3 + 2 + 2
        POOL_TILES = TILES // 2
        POOL_COLS = 9 * P

        def chunk_of(c):
            return slice(c * CHUNK, (c + 1) * CHUNK)

        def adj_moving(g, jt, c):
            if g < FT:
                return AT16[:, PER_CHUNK * c:PER_CHUNK * (c + 1), jt, :]
            return A16[:, jt, chunk_of(c)]

        def uv_slot(c, g):
            return c % 2 if g == 0 else g + 1

        GROUPS = [(Z, 0, 4), (Z, 1, 5), (R, 0, 6), (R, 1, 7), (H, 0, 4), (H, 1, 5)]
        G = len(GROUPS)
        UV = 2 * FT
        TH_BANKS = [(0, 1), (2, 3), (4, 5), (0, 1)]
        OUT_BANKS = [6, 7, 2, 3, 4, 5, 6, 7]
        OWN_BANKS = [6, 7, 4, 5]
        H2_BANKS = [(0, 1), (2, 4), (5, 0), (1, 2)]
        TURNS = [(0, 1), (2, 3), (0, 1), (6, 7)]
        DEG_BANKS = [6, 7, 6, 7, 4, 5, 6, 7]
        X_SLOT = [0, 0, 1, 1]
        DVE_CHUNK = 2
        X_BANKS = [0, 6, 2, 0]
        EARLY = 2
        TURN_AT, COMBINE_AT, SCALE_AT, BACK_AT, LOW_AT = 1, 2, 3, 4, 5

        def unit_at(slot, stage):
            return [slot - stage] if 0 <= slot - stage < UNITS else []

        DEG_SLOTS = {9: 0, 10: 1, 13: 2}
        PRODUCTS = {s: [(2, range(s - 1, s))] for s in range(4, TILES)}
        PRODUCTS[3] = [(2, range(0, 3))]
        for s, piece in enumerate([(0, range(0, 4)), (0, range(4, 8)), (0, range(8, 12)), (0, range(12, TILES)),
                                   (3, range(0, 8)), (1, range(0, 4)), (1, range(4, 8)), (1, [8]),
                                   (1, [9, 10])], 7):
            PRODUCTS[s].append(piece)
        CAST_IN = {s: [s + 1] for s in range(EARLY - 1, 7)}
        CAST_IN[7] = [8, 9]
        CAST_IN.update({s: [s + 2] for s in range(8, TILES - 2)})

        PRODUCTS_LEFT = [(1, range(11, TILES)), (2, [TILES - 1]), (3, range(8, TILES))]

        block = ctx.enter_context(nc.Block())

        @block.sync
        def _(sp):
            for c in range(CHUNKS):
                sp.dma_start(xs[:, 4 * c:4 * c + 4, :],
                             x[chunk_of(c), :].rearrange("(t p) d -> p t d", p=P)).then_inc(x_loaded[c], 16)

            def load_gate_weights():
                for q, src in enumerate((r_W, z_W, h_W)):
                    sp.dma_start(wst[:, 2 * q:2 * q + 2, :],
                                 src.rearrange("(m p) k -> p m k", p=P)).then_inc(weights_loaded, 16)
                for s, (src, b) in enumerate(((in_W, in_b), (out_W, out_b))):
                    sp.dma_start(inw[:, s, :, 0:D],
                                 src.rearrange("(k p) d -> p k d", p=P)).then_inc(weights_loaded, 16)
                    sp.dma_start(inw[:, s, :, D:DB],
                                 b.rearrange("(k p a) -> p k a", p=P, a=1)).then_inc(weights_loaded, 16)

            for it in range(TILES):
                if it >= 2:
                    sp.wait_ge(adj_cast, it - 1)
                sp.dma_start(a_in[:, it % 2, :], adj[it * P:(it + 1) * P, :]).then_inc(adj_loaded[it % 2], 16)
                if it == EARLY - 1:
                    load_gate_weights()
                if it == 3:
                    for q, src in enumerate((r_b, z_b, h_b)):
                        sp.dma_start(gate_b[:, 2 * q:2 * q + 2],
                                     src.rearrange("(m p) -> p m", p=P)).then_inc(biases_loaded, 16)
                    sp.dma_start(o1b[:, :], o1_b.rearrange("(m p) -> p m", p=P)).then_inc(biases_loaded, 16)
            sp.wait_ge(uv_summed, STEPS * CHUNKS * UV)
            for w, src in enumerate((o1_W, w_self, o2_W, w_neigh)):
                sp.dma_start(head_n[:, w, :, :], src.rearrange("(g p) d -> p g d", p=P)).then_inc(head_loaded, 16)
            sp.dma_start(o2b_all, o2_b.rearrange("(a d) -> a d", a=1).broadcast_to([P, D])).then_inc(head_loaded, 16)
            for c in range(CHUNKS):
                sp.dma_start(xr[:, 4 * c:4 * c + 4, :],
                             x[chunk_of(c), :].rearrange("(t p) d -> p t d", p=P)).then_inc(xr_loaded, 16)
            for b in range(2 * CHUNKS):
                sp.wait_ge(out_ready, b + 1)
                sp.dma_start(out[2 * b * P:(2 * b + 2) * P, :].rearrange("(t p) d -> p t d", p=P),
                             x1[:, 2 * b:2 * b + 2, :]).then_inc(stored, 16)
            sp.wait_ge(stored, 16 * 2 * CHUNKS)

        @block.gpsimd
        def _(pool):
            nc.gpsimd.memset(ident[:, :], 0.0).then_inc(ident_zeroed, 1)
            nc.gpsimd.memset(ones16[:, :], 1.0)
            pool.wait_ge(ident_zeroed, 1)
            nc.gpsimd.affine_select(out=ident[:, :], in_=ident[:, :], compare_op=ALU.not_equal, fill=1.0,
                                    base=0, pattern=[[-1, P]], channel_multiplier=1).then_inc(ident_ready, 1)
            pool.wait_ge(ident_ready, 1)
            nc.gpsimd.tensor_copy(ident16[:, :], ident[:, :]).then_inc(ident16_ready, 1)
            nc.gpsimd.memset(deg_out[:, :], 0.0).then_inc(deg_added, 1)
            for it in range(TILES):
                for c in range(DVE_CHUNK):
                    if X_SLOT[c] == it:
                        pool.wait_ge(h0_ready, c + 1)
                        rows = slice(4 * c, 4 * c + 4)
                        nc.gpsimd.tensor_scalar(state_n[:, HI, rows, :], xs[:, rows, :], STATE_SCALE, None,
                                                ALU.mult).then_inc(h0_hi, 1)
                pool.wait_ge(adj_cast, it + 1)
                pool.wait_ge(deg_added, it + 1)
                cols = slice(0, N if it < POOL_TILES else POOL_COLS)
                nc.gpsimd.tensor_tensor(deg_out[:, cols], deg_out[:, cols], A16[:, it, cols],
                                        ALU.add).then_inc(deg_added, 1)
            pool.wait_ge(uv_summed, STEPS * CHUNKS * UV)
            pool.wait_ge(uv_used, STEPS * CHUNKS - 1)
            nc.gpsimd.memset(ones32, 1.0).then_inc(ones_ready, 1)
            pool.wait_ge(head_loaded, 16 * 5)
            pool.wait_ge(xr_loaded, 16 * CHUNKS)
            for t in range(TILES):
                nc.gpsimd.tensor_tensor(xr[:, t, :], xr[:, t, :], o2b_all, ALU.add).then_inc(xb_ready, 1)

        @block.scalar
        def _(act):
            def cast(it):
                act.wait_ge(adj_loaded[it % 2], 16 * (it // 2 + 1))
                if it == TILES - 4:
                    act.wait_ge(x_turned, CHUNKS)
                    act.wait_ge(node_split, 2 * CHUNKS)
                nc.scalar.activation(A16[:, it, :], a_in[:, it % 2, :], ACT.Copy,
                                     accum_out=deg_col[:, it:it + 1]).then_inc(adj_cast, 1)

            for it in range(EARLY):
                cast(it)
                for half in range(2):
                    act.wait_ge(adj_turned, 2 * it + half + 1)
                    nc.scalar.activation(AT16[:, it, 8 * half:8 * half + 8, :],
                                         bank[4 + half].bitcast(F16).rearrange("p (k n) -> p k n", n=P),
                                         ACT.Copy).then_inc(adj_t_ready, 1)
            for it in range(TILES):
                for c in range(DVE_CHUNK):
                    if X_SLOT[c] == it:
                        b = X_BANKS[c]
                        act.wait_ge(x_turned, c + 1)
                        nc.scalar.activation(state_t[:, :, chunk_of(c)], psum[:, b:b + 2, :],
                                             ACT.Copy).then_inc(state_new, FT)
                for ahead in CAST_IN.get(it, ()):
                    cast(ahead)
                for u in unit_at(it, TURN_AT):
                    if u >= 2:
                        act.wait_ge(w_combined, u - 1)
                    act.wait_ge(w_turned, u + 1)
                    nc.scalar.activation(wt[:, u % 2, :, :], bank[0].rearrange("p (k n) -> p k n", k=4),
                                         ACT.Copy).then_inc(wt_ready, 1)
                for u in unit_at(it, COMBINE_AT):
                    act.wait_ge(w_combined, u + 1)
                    nc.scalar.activation(wst[:, u, 0:2 * D].rearrange("p (i d) -> p i d", i=2), psum[:, 6:8, 0:D],
                                         ACT.Copy)
                    nc.scalar.activation(c_gate[:, u, :], psum[:, 6:8, D], ACT.Copy).then_inc(cw_ready, 1)
                for u in unit_at(it, BACK_AT):
                    q, m = divmod(u, FT)
                    act.wait_ge(w_rows_turned, u + 1)
                    cols = slice(m * P, (m + 1) * P)
                    nc.scalar.activation(W16[:, HI, q, 0:4, cols],
                                         bank[1].rearrange("p (k n) -> p k n", n=P), ACT.Copy)
                    nc.scalar.activation(W16[:, HI, q, 4:6, cols],
                                         bank[3][:, 0:2 * P].rearrange("p (k n) -> p k n", n=P),
                                         ACT.Copy).then_inc(w_hi, 1)
                if it in DEG_SLOTS:
                    c = DEG_SLOTS[it]
                    act.wait_ge(deg_maxed, c + 1)
                    nc.scalar.activation(deg_in[:, chunk_of(c)], bank[DEG_BANKS[c]],
                                         ACT.Copy).then_inc(deg_ready, 1)
            for i in range(CHUNKS - 1, 2 * CHUNKS):
                act.wait_ge(deg_maxed, i + 1)
                dst = deg_in[:, chunk_of(i)] if i < CHUNKS else deg_out[:, chunk_of(i - CHUNKS)]
                nc.scalar.activation(dst, bank[DEG_BANKS[i]], ACT.Copy).then_inc(deg_ready, 1)

            def split_state(t, c):
                for f in range(FT):
                    act.wait_ge(state_new, t * (CHUNKS * FT) + FT * c + f + 1)
                    nc.scalar.activation(ss[:, HI, f, :], state_t[:, f, chunk_of(c)], ACT.Copy,
                                         scale=k_scale[:, 0:1]).then_inc(s_hi, 1)

            def split_uv(t, c, g):
                act.wait_ge(uv_summed, t * (CHUNKS * UV) + UV * c + g + 1)
                user = c - 1 if g == 0 else c
                if user >= 1:
                    act.wait_ge(uv_used, t * CHUNKS + user)
                nc.scalar.activation(uv[:, uv_slot(c, g), HI, :], bank[g], ACT.Copy,
                                     scale=u_scale[:, 0:1]).then_inc(uv_hi, 1)

            def split_nodes(t, c):
                for j, b in enumerate(TURNS[c]):
                    act.wait_ge(turned, t * (2 * CHUNKS) + 2 * c + j + 1)
                    nc.scalar.activation(state_n[:, HI, 4 * c + 2 * j:4 * c + 2 * j + 2, :],
                                         bank[b].rearrange("p (t d) -> p t d", d=D), ACT.Copy,
                                         scale=STATE_SCALE).then_inc(node_hi, 1)

            def switch_on(t, c, n):
                q, m, b = GROUPS[n]
                u = FT * q + m
                act.wait_ge(gate_biased, t * (CHUNKS * G) + G * c + n + 1)
                dst = zt[:, m, :] if q == Z else bank[b]
                nc.scalar.activation(dst, bank[b], ACT.Tanh if q == H else ACT.Sigmoid,
                                     bias=gate_b[:, u:u + 1], scale=inv[:, u:u + 1]).then_inc(gate_on, 1)

            def split_rs(t, c):
                act.wait_ge(gate_summed, t * (CHUNKS * G) + G * c + 4)
                for f in range(FT):
                    act.wait_ge(rs_ready, t * (CHUNKS * FT) + FT * c + f + 1)
                    nc.scalar.activation(ss[:, HI, f, :], bank[6 + f], ACT.Copy,
                                         scale=k_scale[:, 0:1]).then_inc(rs_hi, 1)

            def split_final(c):
                act.wait_ge(state_new, STEPS * CHUNKS * FT + FT * (c + 1))
                nc.scalar.activation(fin[:, c, HI, :, :], state_t[:, :, chunk_of(c)], ACT.Copy,
                                     scale=STATE_SCALE).then_inc(final_hi, 1)

            def turned_heads():
                act.wait_ge(head_scaled, 1)
                for w in (O1, SELF):
                    act.wait_ge(head_turned, w + 1)
                    nc.scalar.activation(head_t[:, HI, w, :, :], bank[w].rearrange("p (k d) -> p k d", k=FT),
                                         ACT.Copy, scale=head_scale[:, w:w + 1]).then_inc(head_hi, 1)
                act.wait_ge(head_turned, O2 + 1)
                nc.scalar.activation(o2_t, bank[O2].rearrange("p (k d) -> p k d", k=FT),
                                     ACT.Copy).then_inc(o2_ready, 1)

            def turned_neigh():
                act.wait_ge(head_turned, NEIGH + 1)
                act.wait_ge(uv_used, STEPS * CHUNKS)
                nc.scalar.activation(neigh_t, bank[NEIGH].rearrange("p (k d) -> p k d", k=FT),
                                     ACT.Copy).then_inc(neigh_ready, 1)

            def hidden_on(c):
                for g, b in enumerate(TH_BANKS[c]):
                    act.wait_ge(th_summed, FT * c + g + 1)
                    nc.scalar.activation(th[:, g, chunk_of(c)], bank[b], ACT.Tanh, bias=o1b[:, g:g + 1],
                                         scale=head_inv[:, O1:O1 + 1]).then_inc(th_ready, 1)

            def step(t, final):
                for c in range(CHUNKS):
                    last = c == CHUNKS - 1
                    if not last:
                        split_uv(t, c + 1, 0)
                    for n in range(4):
                        switch_on(t, c, n)
                        if last and n < 3 and not final:
                            split_nodes(t, n)
                        if last and n < 2 and final:
                            split_final(n)
                    if last and final:
                        turned_heads()
                    split_rs(t, c)
                    if not last:
                        split_uv(t, c + 1, 1)
                    elif final:
                        split_final(2)
                        turned_neigh()
                        hidden_on(0)
                    switch_on(t, c, 4)
                    switch_on(t, c, 5)
                    if not last:
                        split_state(t, c + 1)
                        split_uv(t, c + 1, 2)
                        split_uv(t, c + 1, 3)
                if not final:
                    split_state(t + 1, 0)
                    split_nodes(t, CHUNKS - 1)
                    for g in range(UV):
                        split_uv(t + 1, 0, g)

            act.wait_ge(u_scale_ready, 1)
            for g in range(UV):
                split_uv(0, 0, g)
            act.wait_ge(scales_ready, 1)
            act.wait_ge(biases_loaded, 16 * 4)
            split_state(0, 0)
            with act.Fori(0, STEPS - 1) as t:
                step(t, False)
            step(STEPS - 1, True)

            hidden_on(1)
            split_final(CHUNKS - 1)
            hidden_on(2)
            hidden_on(3)
            def normalise(c):
                act.wait_ge(norm_ready, c // 2 + 1)
                for j in range(4 * c, 4 * c + 4):
                    ins = nc.scalar.activation(h2[:, j, :], x1[:, j, :], ACT.Relu, bias=shift[:, j:j + 1],
                                               scale=rstd[:, j:j + 1])
                ins.then_inc(h2_ready, 1)

            def turned_h2(c):
                for f, b in enumerate(H2_BANKS[c]):
                    act.wait_ge(h2_turned, FT * c + f + 1)
                    nc.scalar.activation(h2t[:, HI, f, chunk_of(c)], bank[b], ACT.Copy,
                                         scale=STATE_SCALE).then_inc(h2t_hi, 1)

            def park(c):
                act.wait_ge(h2col_ready, c + 1)
                for b in range(2 * c, 2 * c + 2):
                    act.wait_ge(self_summed, b + 1)
                    nc.scalar.activation(h2[:, 2 * b:2 * b + 2, :],
                                         bank[OWN_BANKS[b % 4]].rearrange("p (t d) -> p t d", d=D),
                                         ACT.Copy, scale=head_inv[:, SELF:SELF + 1]).then_inc(self_parked, 1)

            normalise(0)
            normalise(1)
            turned_h2(0)
            act.wait_ge(wsum_summed, 1)
            nc.scalar.activation(wsum_all, bank[3][:, 0:D], ACT.Copy).then_inc(wsum_ready, 1)
            turned_h2(1)
            normalise(2)
            normalise(3)
            park(0)
            turned_h2(2)
            turned_h2(3)
            for c in range(1, CHUNKS):
                park(c)

        @block.vector
        def _(dve):
            chain = [0]

            def link(ins):
                chain[0] += 1
                ins.then_inc(dve_chain, 1)
                dve.wait_ge(dve_chain, chain[0])

            def inverse_root(sl):
                nc.vector.tensor_scalar(half_v[:, sl], mv[:, sl, 1], EPS, -0.5, ALU.add, ALU.mult)
                link(nc.vector.tensor_scalar(tmp[:, sl], mv[:, sl, 1], EPS, None, ALU.add))
                link(nc.vector.tensor_scalar(rstd[:, sl].bitcast(I32), tmp[:, sl].bitcast(I32), 1, None,
                                             ALU.logical_shift_right))
                link(nc.vector.tensor_scalar(rstd[:, sl].bitcast(I32), rstd[:, sl].bitcast(I32), -1.0,
                                             float(RSQRT_GUESS), ALU.mult, ALU.add))
                for _ in range(3):
                    link(nc.vector.tensor_tensor(tmp[:, sl], rstd[:, sl], rstd[:, sl], ALU.mult))
                    link(nc.vector.tensor_tensor(tmp[:, sl], tmp[:, sl], half_v[:, sl], ALU.mult))
                    link(nc.vector.scalar_tensor_tensor(rstd[:, sl], tmp[:, sl], 1.5, rstd[:, sl],
                                                        ALU.add, ALU.mult))

            def power_of_two(dst, src, exponent):
                link(nc.vector.tensor_scalar(dst.bitcast(I32), src.bitcast(I32), EXP_MASK, None, ALU.bitwise_and))
                link(nc.vector.tensor_scalar(dst.bitcast(I32), dst.bitcast(I32), -1.0, (exponent + 254) * MANT,
                                             ALU.mult, ALU.add))

            for c in range(CHUNKS):
                dve.wait_ge(x_loaded[c], 16)
                if c >= 1:
                    dve.wait_ge(dve_chain, chain[0])
                for j in range(4):
                    ins = nc.vector.bn_stats(stats[:, j, :], xs[:, 4 * c + j, :])
                link(ins)
                for j in range(4):
                    ins = nc.vector.bn_aggr(mv[:, 4 * c + j, :], stats[:, j, :])
                link(ins)
            inverse_root(slice(0, TILES))
            for c in range(CHUNKS):
                for j in range(4 * c, 4 * c + 4):
                    ins = nc.vector.tensor_scalar(xs[:, j, :], xs[:, j, :], mv[:, j, 0:1], rstd[:, j:j + 1],
                                                  ALU.subtract, ALU.mult)
                link(ins)
                nc.vector.tensor_scalar(xs[:, 4 * c:4 * c + 4, :], xs[:, 4 * c:4 * c + 4, :], 0.0, None,
                                        ALU.max).then_inc(h0_ready, 1)
            dve.wait_ge(ident16_ready, 1)
            for it in range(TILES):
                if it == 1:
                    for c in range(DVE_CHUNK, CHUNKS):
                        b = X_BANKS[c]
                        dve.wait_ge(x_turned, c + 1)
                        dve.wait_ge(state_new, FT * c)
                        nc.vector.tensor_copy(state_t[:, :, chunk_of(c)], psum[:, b:b + 2, :]).then_inc(state_new, FT)
                    for c in range(DVE_CHUNK, CHUNKS):
                        rows = slice(4 * c, 4 * c + 4)
                        nc.vector.tensor_scalar(state_n[:, HI, rows, :], xs[:, rows, :], STATE_SCALE, None,
                                                ALU.mult).then_inc(h0_hi_own, 1)
                    for c in range(CHUNKS):
                        if c < DVE_CHUNK:
                            dve.wait_ge(h0_hi, c + 1)
                        else:
                            dve.wait_ge(h0_hi_own, c - DVE_CHUNK + 1)
                        rows = slice(4 * c, 4 * c + 4)
                        nc.vector.scalar_tensor_tensor(state_n[:, LO, rows, :], xs[:, rows, :], STATE_SCALE,
                                                       state_n[:, HI, rows, :],
                                                       ALU.mult, ALU.subtract).then_inc(node_split, 2)
                for u in unit_at(it, LOW_AT):
                    q, m = divmod(u, FT)
                    cols = slice(m * P, (m + 1) * P)
                    dve.wait_ge(w_hi, u + 1)
                    nc.vector.tensor_tensor(W16[:, LO, q, 0:4, cols],
                                            bank[1].rearrange("p (k n) -> p k n", n=P),
                                            W16[:, HI, q, 0:4, cols], ALU.subtract)
                    nc.vector.tensor_tensor(W16[:, LO, q, 4:6, cols],
                                            bank[3][:, 0:2 * P].rearrange("p (k n) -> p k n", n=P),
                                            W16[:, HI, q, 4:6, cols], ALU.subtract).then_inc(w_split, 1)
                for u in unit_at(it, SCALE_AT):
                    dve.wait_ge(cw_ready, u + 1)
                    link(nc.vector.tensor_reduce(rowmax[:, u:u + 1], wst[:, u, :], AX.X, ALU.max,
                                                 apply_absolute_value=True))
                    link(nc.vector.tensor_scalar(rowmax[:, u:u + 1], rowmax[:, u:u + 1], 2.0 ** -100, None,
                                                 ALU.max))
                    power_of_two(sigma[:, u:u + 1], rowmax[:, u:u + 1], 14)
                    nc.vector.tensor_scalar(wst[:, u, :], wst[:, u, :], sigma[:, u:u + 1], None,
                                            ALU.mult).then_inc(w_scaled, 1)
                dve.wait_ge(adj_cast, it + 1)
                nc.vector.tensor_scalar(deg_in[:, it * P:(it + 1) * P], ident16[:, :], deg_col[:, it:it + 1], None,
                                        ALU.mult).then_inc(diag_ready, 1)
                if it >= POOL_TILES:
                    if it == POOL_TILES:
                        dve.wait_ge(deg_added, POOL_TILES + 1)
                    else:
                        dve.wait_ge(deg_half_added, it - POOL_TILES)
                    cols = slice(POOL_COLS, N)
                    nc.vector.tensor_tensor(deg_out[:, cols], deg_out[:, cols], A16[:, it, cols],
                                            ALU.add).then_inc(deg_half_added, 1)
                if it == 9:
                    dve.wait_ge(w_rows_turned, UNITS)
                for half in range(2 if it >= EARLY else 0):
                    dve.wait_ge(adj_turned, 2 * it + half + 1)
                    nc.vector.tensor_copy(AT16[:, it, 8 * half:8 * half + 8, :],
                                          bank[4 + half].bitcast(F16).rearrange("p (k n) -> p k n", n=P)
                                          ).then_inc(adj_t_ready, 1)
                if it in DEG_SLOTS:
                    c = DEG_SLOTS[it]
                    dve.wait_ge(deg_summed, c + 1)
                    nc.vector.tensor_reduce(dmax[:, c:c + 1], bank[DEG_BANKS[c]], AX.X,
                                            ALU.max).then_inc(deg_maxed, 1)
            for i in range(CHUNKS - 1, 2 * CHUNKS):
                dve.wait_ge(deg_summed, i + 1)
                nc.vector.tensor_reduce(dmax[:, i:i + 1], bank[DEG_BANKS[i]], AX.X,
                                        ALU.max).then_inc(deg_maxed, 1)
            dve.wait_ge(deg_maxed, 2 * CHUNKS)
            link(nc.vector.tensor_reduce(dtop[:, :], dmax[:, :], AX.X, ALU.max))
            link(nc.vector.tensor_scalar(dtop[:, :], dtop[:, :], 1.0, None, ALU.max))
            power_of_two(k_scale[:, 0:1], dtop[:, 0:1], 10)
            nc.vector.tensor_scalar(u_scale[:, 0:1], k_scale[:, 0:1], 1.0 / STATE_SCALE, None,
                                    ALU.mult).then_inc(u_scale_ready, 1)
            link(nc.vector.tensor_scalar(sigma[:, :], sigma[:, :], k_scale[:, 0:1], None, ALU.mult))
            for s in range(2):
                link(nc.vector.tensor_tensor(c_gate[:, :, s], c_gate[:, :, s], sigma[:, :], ALU.mult))
            nc.vector.reciprocal(inv[:, :], sigma[:, :]).then_inc(scales_ready, 1)

            def split_final(c):
                dve.wait_ge(final_hi, c + 1)
                nc.vector.scalar_tensor_tensor(fin[:, c, LO, :, :], state_t[:, :, chunk_of(c)], STATE_SCALE,
                                               fin[:, c, HI, :, :], ALU.mult, ALU.subtract).then_inc(final_split, 1)

            def max_heads():
                dve.wait_ge(head_loaded, 16 * 5)
                nc.vector.tensor_reduce(head_max, head_n[:, 0:2, :, :].rearrange("p w g d -> p w (g d)"), AX.X,
                                        ALU.max, apply_absolute_value=True).then_inc(head_maxed, 1)

            def scale_heads():
                dve.wait_ge(head_max_summed, 1)
                link(nc.vector.tensor_scalar(head_max, bank[3][:, 0:2], 2.0 ** -100, None, ALU.max))
                power_of_two(head_scale, head_max, 14)
                link(nc.vector.reciprocal(head_inv, head_scale))
                nc.vector.tensor_scalar(head_inv, head_inv, 1.0 / STATE_SCALE, None, ALU.mult).then_inc(head_scaled, 1)

            def split_heads():
                for w in (O1, SELF):
                    dve.wait_ge(head_hi, w + 1)
                    nc.vector.scalar_tensor_tensor(head_t[:, LO, w, :, :], bank[w].rearrange("p (k d) -> p k d", k=FT),
                                                   head_scale[:, w:w + 1], head_t[:, HI, w, :, :],
                                                   ALU.mult, ALU.subtract).then_inc(head_split, 1)

            LINKS = CHUNKS * (G + 2 * FT)
            links = [0]

            def step_link(t, ins):
                links[0] += 1
                ins.then_inc(step_chain, 1)
                dve.wait_ge(step_chain, t * LINKS + links[0])

            def split_state(t, c):
                for f in range(FT):
                    dve.wait_ge(s_hi, t * (CHUNKS * FT) + FT * c + f + 1)
                    nc.vector.scalar_tensor_tensor(ss[:, LO, f, :], state_t[:, f, chunk_of(c)],
                                                   k_scale[:, 0:1], ss[:, HI, f, :],
                                                   ALU.mult, ALU.subtract).then_inc(s_split, 1)

            def split_uv(t, c, g):
                dve.wait_ge(uv_hi, t * (CHUNKS * UV) + UV * c + g + 1)
                slot = uv_slot(c, g)
                nc.vector.scalar_tensor_tensor(uv[:, slot, LO, :], bank[g], u_scale[:, 0:1],
                                               uv[:, slot, HI, :], ALU.mult, ALU.subtract).then_inc(uv_split, 1)

            def split_nodes(t, c):
                for j, b in enumerate(TURNS[c]):
                    dve.wait_ge(node_hi, t * (2 * CHUNKS) + 2 * c + j + 1)
                    rows = slice(4 * c + 2 * j, 4 * c + 2 * j + 2)
                    nc.vector.scalar_tensor_tensor(state_n[:, LO, rows, :],
                                                   bank[b].rearrange("p (t d) -> p t d", d=D),
                                                   STATE_SCALE, state_n[:, HI, rows, :],
                                                   ALU.mult, ALU.subtract).then_inc(node_split, 1)

            def add_degrees(t, c, n):
                q, m, b = GROUPS[n]
                u = FT * q + m
                dve.wait_ge(gate_summed, t * (CHUNKS * G) + G * c + n + 1)
                step_link(t, nc.vector.scalar_tensor_tensor(bank[b], deg_in[:, chunk_of(c)],
                                                            c_gate[:, u, 0:1], bank[b], ALU.mult, ALU.add))
                nc.vector.scalar_tensor_tensor(bank[b], deg_out[:, chunk_of(c)], c_gate[:, u, 1:2],
                                               bank[b], ALU.mult, ALU.add).then_inc(gate_biased, 1)

            def reset_state(t, c, f):
                dve.wait_ge(gate_on, t * (CHUNKS * G) + G * c + 2 + f + 1)
                nc.vector.tensor_tensor(bank[6 + f], bank[6 + f], state_t[:, f, chunk_of(c)],
                                        ALU.mult).then_inc(rs_ready, 1)

            def split_rs(t, c):
                for f in range(FT):
                    dve.wait_ge(rs_hi, t * (CHUNKS * FT) + FT * c + f + 1)
                    nc.vector.scalar_tensor_tensor(ss[:, LO, f, :], bank[6 + f], k_scale[:, 0:1],
                                                   ss[:, HI, f, :], ALU.mult, ALU.subtract).then_inc(rs_split, 1)

            def update(t, c, f):
                dve.wait_ge(gate_on, t * (CHUNKS * G) + G * c + 4 + f + 1)
                h = bank[4 + f]
                st = state_t[:, f, chunk_of(c)]
                step_link(t, nc.vector.tensor_tensor(h, h, st, ALU.subtract))
                step_link(t, nc.vector.tensor_tensor(h, h, zt[:, f, :], ALU.mult))
                nc.vector.tensor_tensor(st, h, st, ALU.add).then_inc(state_new, 1)

            def step(t, final):
                links[0] = 0
                for c in range(CHUNKS):
                    last = c == CHUNKS - 1
                    if not last:
                        split_uv(t, c + 1, 0)
                    for n in range(4):
                        if last and n == 3 and final:
                            scale_heads()
                        add_degrees(t, c, n)
                        if n >= 2:
                            reset_state(t, c, n - 2)
                        if last and n < 3 and not final:
                            split_nodes(t, n)
                        if last and n < 2 and final:
                            split_final(n)
                        if last and n == 1 and final:
                            max_heads()
                    if last and final:
                        split_heads()
                    split_rs(t, c)
                    if not last:
                        split_uv(t, c + 1, 1)
                    elif final:
                        split_final(2)
                    add_degrees(t, c, 4)
                    add_degrees(t, c, 5)
                    update(t, c, 0)
                    update(t, c, 1)
                    if not last:
                        split_state(t, c + 1)
                        split_uv(t, c + 1, 2)
                        split_uv(t, c + 1, 3)
                if not final:
                    split_state(t + 1, 0)
                    split_nodes(t, CHUNKS - 1)
                    for g in range(UV):
                        split_uv(t + 1, 0, g)

            dve.wait_ge(u_scale_ready, 1)
            for g in range(UV):
                split_uv(0, 0, g)
            split_state(0, 0)
            with dve.Fori(0, STEPS - 1) as t:
                step(t, False)
            step(STEPS - 1, True)

            def first_layer(c):
                for j in range(2):
                    b = 2 * c + j
                    dve.wait_ge(xb_ready, 2 * b + 2)
                    dve.wait_ge(o2_summed, b + 1)
                    rows = slice(2 * b, 2 * b + 2)
                    nc.vector.tensor_tensor(x1[:, rows, :], bank[OUT_BANKS[b]].rearrange("p (t d) -> p t d", d=D),
                                            xr[:, rows, :], ALU.add).then_inc(o2_taken, 1)
                dve.wait_ge(o2_taken, 2 * c + 2)
                for j in range(4):
                    ins = nc.vector.bn_stats(stats[:, j, :], x1[:, 4 * c + j, :])
                link(ins)
                for j in range(4):
                    ins = nc.vector.bn_aggr(mv[:, 4 * c + j, :], stats[:, j, :])
                link(ins)

            def norms(pair):
                sl = slice(8 * pair, 8 * pair + 8)
                inverse_root(sl)
                nc.vector.scalar_tensor_tensor(shift[:, sl], mv[:, sl, 0], -1.0, rstd[:, sl],
                                               ALU.mult, ALU.mult).then_inc(norm_ready, 1)

            def split_column(c):
                sl = slice(4 * c, 4 * c + 4)
                dve.wait_ge(h2_ready, c + 1)
                link(nc.vector.tensor_scalar(h2col[:, sl, 0], h2[:, sl, 0], STATE_SCALE, None, ALU.mult))
                nc.vector.scalar_tensor_tensor(h2col[:, sl, 1], h2[:, sl, 0], STATE_SCALE, h2col[:, sl, 0],
                                               ALU.mult, ALU.subtract).then_inc(h2col_ready, 1)

            def split_h2(c):
                for f, b in enumerate(H2_BANKS[c]):
                    dve.wait_ge(h2t_hi, FT * c + f + 1)
                    nc.vector.scalar_tensor_tensor(h2t[:, LO, f, chunk_of(c)], bank[b], STATE_SCALE,
                                                   h2t[:, HI, f, chunk_of(c)],
                                                   ALU.mult, ALU.subtract).then_inc(h2t_split, 1)

            split_final(CHUNKS - 1)
            first_layer(0)
            first_layer(1)
            norms(0)
            first_layer(2)
            split_column(0)
            first_layer(3)
            split_column(1)
            norms(1)
            split_h2(0)
            split_h2(1)
            split_column(2)
            split_column(3)
            split_h2(2)
            split_h2(3)
            nc.vector.tensor_scalar(deg_col[:, :], deg_col[:, :], 0.0, 1.0 / STATE_SCALE, ALU.is_gt, ALU.mult)
            dve.wait_ge(s_summed, 1)
            link(nc.vector.tensor_reduce(s_col[:, :], bank[3][:, 0:2 * TILES].rearrange("p (t s) -> p t s", s=2),
                                         AX.X, ALU.add))
            link(nc.vector.tensor_tensor(s_col[:, :], s_col[:, :], deg_col[:, :], ALU.mult))
            dve.wait_ge(wsum_ready, 1)
            flat = "p t d -> p (t d)"
            def add_neighbours(b):
                dve.wait_ge(self_parked, b + 1)
                for n in (2 * b, 2 * b + 1):
                    ins = nc.vector.scalar_tensor_tensor(h2[:, n, :], wsum_all, s_col[:, n:n + 1], h2[:, n, :],
                                                         ALU.mult, ALU.add)
                ins.then_inc(both_added, 1)

            add_neighbours(0)
            for b in range(2 * CHUNKS):
                if b + 1 < 2 * CHUNKS:
                    add_neighbours(b + 1)
                dve.wait_ge(both_added, b + 1)
                rows = slice(2 * b, 2 * b + 2)
                nc.vector.scalar_tensor_tensor(x1[:, rows, :].rearrange(flat), h2[:, rows, :].rearrange(flat), 0.0,
                                               x1[:, rows, :].rearrange(flat), ALU.max, ALU.add).then_inc(out_ready, 1)

        @block.tensor
        def _(pe):
            mm = nc.tensor.matmul

            def sum_group(c, g, tiles):
                f = g % FT
                for jt in tiles:
                    for part in (HI, LO):
                        last = mm(bank[g], state_n[:, part, jt, f * P:(f + 1) * P], adj_moving(g, jt, c),
                                  start=(jt == 0 and part == HI), stop=(jt == TILES - 1 and part == LO))
                if tiles[-1] == TILES - 1:
                    last.then_inc(uv_summed, 1)

            def turn_adj(it):
                pe.wait_ge(adj_cast, it + 1)
                for half in range(2):
                    if it >= 1:
                        pe.wait_ge(adj_t_ready, 2 * it + half - 1)
                    for k in range(8):
                        jt = 8 * half + k
                        last = nc.tensor.transpose(bank[4 + half].bitcast(F16)[:, k * P:(k + 1) * P],
                                                   A16[:, it, jt * P:(jt + 1) * P], ident16[:, :])
                    last.then_inc(adj_turned, 1)

            pe.wait_ge(ident16_ready, 1)
            for it in range(EARLY):
                turn_adj(it)
            for it in range(TILES):
                if it in DEG_SLOTS:
                    c = DEG_SLOTS[it]
                    pe.wait_ge(diag_ready, 4 * (c + 1))
                    if c == 0:
                        pe.wait_ge(cw_ready, UNITS)
                    elif c == 2:
                        pe.wait_ge(deg_ready, 1)
                    mm(bank[DEG_BANKS[c]], ones16[:, :], deg_in[:, chunk_of(c)],
                       start=True, stop=True).then_inc(deg_summed, 1)
                for c in range(CHUNKS):
                    if X_SLOT[c] == it:
                        pe.wait_ge(h0_ready, c + 1)
                        if c == 3:
                            pe.wait_ge(state_new, FT)
                        for f in range(FT):
                            for j in range(4):
                                last = nc.tensor.transpose(bank[X_BANKS[c] + f][:, j * P:(j + 1) * P],
                                                           xs[:, 4 * c + j, f * P:(f + 1) * P], ident[:, :])
                        last.then_inc(x_turned, 1)
                for u in unit_at(it, TURN_AT):
                    if u == 0:
                        pe.wait_ge(weights_loaded, 16 * N_WEIGHT_DMAS)
                        pe.wait_ge(state_new, FT * CHUNKS)
                    else:
                        pe.wait_ge(wt_ready, u)
                    for k in range(4):
                        last = nc.tensor.transpose(bank[0][:, k * P:(k + 1) * P], wst[:, u, k * P:(k + 1) * P],
                                                   ident[:, :])
                    last.then_inc(w_turned, 1)
                for u in unit_at(it, COMBINE_AT):
                    pe.wait_ge(wt_ready, u + 1)
                    if u >= 1:
                        pe.wait_ge(cw_ready, u)
                    for i in range(2):
                        for k in range(FT):
                            last = mm(bank[6 + i][:, 0:DB], wt[:, u % 2, FT * i + k, :], inw[:, i, k, :],
                                      start=(k == 0), stop=(k == FT - 1))
                    last.then_inc(w_combined, 1)
                if it == 3:
                    pe.wait_ge(node_split, 2 * CHUNKS)
                if it == 11:
                    pe.wait_ge(w_split, UNITS)
                for g, tiles in PRODUCTS.get(it, ()):
                    sum_group(0, g, tiles)
                for u in unit_at(it, BACK_AT):
                    pe.wait_ge(w_scaled, u + 1)
                    if u >= 1:
                        pe.wait_ge(w_split, u)
                    for k in range(KT):
                        last = nc.tensor.transpose(bank[(1, 3)[k // 4]][:, (k % 4) * P:(k % 4 + 1) * P],
                                                   wst[:, u, k * P:(k + 1) * P], ident[:, :])
                    last.then_inc(w_rows_turned, 1)
                if it >= EARLY:
                    turn_adj(it)
            pe.wait_ge(diag_ready, TILES)
            pe.wait_ge(deg_ready, CHUNKS - 1)
            for i in (3, 4, 5, 6, 7):
                if i == 4:
                    for g, tiles in PRODUCTS_LEFT[:1]:
                        sum_group(0, g, tiles)
                    pe.wait_ge(deg_added, TILES + 1)
                    pe.wait_ge(deg_half_added, TILES - POOL_TILES)
                    pe.wait_ge(adj_t_ready, 2 * TILES)
                if i == 7:
                    pe.wait_ge(deg_ready, CHUNKS)
                src = deg_in[:, chunk_of(i)] if i < CHUNKS else deg_out[:, chunk_of(i - CHUNKS)]
                mm(bank[DEG_BANKS[i]], ones16[:, :], src, start=True, stop=True).then_inc(deg_summed, 1)
            for g, tiles in PRODUCTS_LEFT[1:]:
                sum_group(0, g, tiles)
            pe.wait_ge(deg_ready, 2 * CHUNKS)

            def whole_group(t, c, g):
                pe.wait_ge(uv_split, t * (CHUNKS * UV) + UV * (c - 1) + g + 1)
                sum_group(c, g, range(TILES))

            def gate_terms(t, c, n, kts, first, final):
                q, m, b = GROUPS[n]
                for i, k in enumerate(kts):
                    if n == 0 and k < UV:
                        pe.wait_ge(uv_split, t * (CHUNKS * UV) + UV * c + k + 1)
                    for j, (wp, xp) in enumerate(((HI, HI), (LO, HI), (HI, LO))):
                        src = uv[:, uv_slot(c, k), xp, :] if k < UV else ss[:, xp, k - UV, :]
                        last = mm(bank[b], W16[:, wp, q, k, m * P:(m + 1) * P], src,
                                  start=(first and i == 0 and j == 0),
                                  stop=(final and i == len(kts) - 1 and j == 2))
                return last

            def gates_rz(t, c, n):
                if n < 2:
                    pe.wait_ge(state_new, (t + 1) * (CHUNKS * FT) + FT * c + n - 1)
                if n == 0:
                    pe.wait_ge(s_split, t * (CHUNKS * FT) + FT * (c + 1))
                gate_terms(t, c, n, (4, 5, 0, 1, 2, 3), True, True).then_inc(gate_summed, 1)

            def gates_h_uv(t, c):
                for n in (4, 5):
                    pe.wait_ge(gate_on, t * (CHUNKS * G) + G * c + n - 3)
                    last = gate_terms(t, c, n, (0, 1, 2, 3), True, False)
                last.then_inc(uv_used, 1)

            def gates_h_rs(t, c):
                for n in (4, 5):
                    for f in range(FT):
                        pe.wait_ge(rs_split, t * (CHUNKS * FT) + FT * c + f + 1)
                        last = gate_terms(t, c, n, (UV + f,), False, f == FT - 1)
                    last.then_inc(gate_summed, 1)

            def turn(t, c):
                pe.wait_ge(state_new, (t + 1) * (CHUNKS * FT) + FT * (c + 1))
                for j, b in enumerate(TURNS[c]):
                    for k in range(2):
                        for f in range(FT):
                            jt = 4 * c + 2 * j + k
                            last = nc.tensor.transpose(bank[b][:, k * D + f * P:k * D + (f + 1) * P],
                                                       state_t[:, f, jt * P:(jt + 1) * P], ident[:, :])
                    last.then_inc(turned, 1)

            def turn_heads():
                pe.wait_ge(uv_split, STEPS * CHUNKS * UV)
                pe.wait_ge(head_loaded, 16 * 5)
                pe.wait_ge(head_maxed, 1)
                pe.wait_ge(ones_ready, 1)
                mm(bank[3][:, 0:2], ones32, head_max, start=True, stop=True).then_inc(head_max_summed, 1)
                for w in range(3):
                    turn_head(w)

            def turn_head(w):
                for k in range(FT):
                    for g in range(FT):
                        last = nc.tensor.transpose(bank[w][:, k * D + g * P:k * D + (g + 1) * P],
                                                   head_n[:, w, g, k * P:(k + 1) * P], ident[:, :])
                last.then_inc(head_turned, 1)

            def first_layer_hidden(c):
                pe.wait_ge(head_split, 2)
                if c == 1:
                    pe.wait_ge(o2_ready, 1)
                    pe.wait_ge(neigh_ready, 1)
                pe.wait_ge(final_split, c + 1)
                if c == 2:
                    pe.wait_ge(state_new, (STEPS + 1) * (CHUNKS * FT))
                if c == 3:
                    pe.wait_ge(th_ready, FT)
                for g, b in enumerate(TH_BANKS[c]):
                    for k in range(FT):
                        for j, (wp, xp) in enumerate(((HI, HI), (LO, HI), (HI, LO))):
                            last = mm(bank[b], head_t[:, wp, O1, k, g * P:(g + 1) * P], fin[:, c, xp, k, :],
                                      start=(k == 0 and j == 0), stop=(k == FT - 1 and j == 2))
                    last.then_inc(th_summed, 1)

            def step(t, final):
                for c in range(CHUNKS):
                    last_chunk = c == CHUNKS - 1
                    if not last_chunk:
                        whole_group(t, c + 1, 0)
                    for n in range(4):
                        gates_rz(t, c, n)
                        if last_chunk and n < 3 and not final:
                            if n == 0:
                                pe.wait_ge(uv_split, t * (CHUNKS * UV) + UV * c + 2)
                            elif n == 1:
                                pe.wait_ge(uv_split, t * (CHUNKS * UV) + UV * c + 4)
                            else:
                                pe.wait_ge(node_split, (t + 1) * (2 * CHUNKS) + 2)
                            turn(t, n)
                    if last_chunk and final:
                        turn_heads()
                    gates_h_uv(t, c)
                    if not last_chunk:
                        whole_group(t, c + 1, 1)
                    elif final:
                        pe.wait_ge(head_scaled, 1)
                        turn_head(NEIGH)
                        first_layer_hidden(0)
                    gates_h_rs(t, c)
                    if not last_chunk:
                        whole_group(t, c + 1, 2)
                        whole_group(t, c + 1, 3)
                if not final:
                    pe.wait_ge(node_split, (t + 1) * (2 * CHUNKS) + 2 * (CHUNKS - 1))
                    for g in range(UV):
                        if g == UV - 1:
                            turn(t, CHUNKS - 1)
                        sum_group(0, g, range(0, TILES - 4))
                    pe.wait_ge(node_split, (t + 2) * (2 * CHUNKS))
                    for g in range(UV):
                        sum_group(0, g, range(TILES - 4, TILES))

            with pe.Fori(0, STEPS - 1) as t:
                step(t, False)
            step(STEPS - 1, True)

            def first_layer_out(c):
                pe.wait_ge(th_ready, FT * (c + 1))
                for j in range(2):
                    b = 2 * c + j
                    if b >= 6:
                        pe.wait_ge(o2_taken, b - 5)
                    for i in range(2):
                        n = 2 * b + i
                        for k in range(FT):
                            last = mm(bank[OUT_BANKS[b]][:, i * D:(i + 1) * D], th[:, k, n * P:(n + 1) * P],
                                      o2_t[:, k, :], start=(k == 0), stop=(k == FT - 1))
                    last.then_inc(o2_summed, 1)

            def turn_h2(c):
                pe.wait_ge(h2_ready, c + 1)
                for f, b in enumerate(H2_BANKS[c]):
                    if c < 3 and b in OUT_BANKS:
                        pe.wait_ge(o2_taken, OUT_BANKS.index(b) + 1)
                    elif c >= 2:
                        pe.wait_ge(h2t_split, FT * (c - 2) + f)
                    for j in range(4):
                        last = nc.tensor.transpose(bank[b][:, j * P:(j + 1) * P],
                                                   h2[:, 4 * c + j, f * P:(f + 1) * P], ident[:, :])
                    last.then_inc(h2_turned, 1)

            def sum_neighbours(c):
                pe.wait_ge(h2col_ready, c + 1)
                for jt in range(4 * c, 4 * c + 4):
                    for it in range(TILES):
                        last = mm(bank[3][:, 2 * it:2 * it + 2], AT16[:, it, jt, :], h2col[:, jt, :],
                                  start=(jt == 0 and it == 0), stop=(jt == TILES - 1), skip_group_check=True)
                if c == CHUNKS - 1:
                    last.then_inc(s_summed, 1)

            def own_term(c):
                pe.wait_ge(h2t_split, FT * (c + 1))
                if c == 1:
                    pe.wait_ge(h2t_split, 5)
                for j in range(2):
                    b = 2 * c + j
                    if b < 2:
                        pe.wait_ge(o2_taken, 6 + b + 1)
                    elif b >= 4:
                        pe.wait_ge(self_parked, b - 3)
                    for i in range(2):
                        n = 2 * b + i
                        for k in range(FT):
                            for part, (wp, xp) in enumerate(((HI, HI), (HI, LO), (LO, HI))):
                                last = mm(bank[OWN_BANKS[b % 4]][:, i * D:(i + 1) * D],
                                          h2t[:, xp, k, n * P:(n + 1) * P], head_t[:, wp, SELF, k, :],
                                          start=(k == 0 and part == 0), stop=(k == FT - 1 and part == 2))
                    last.then_inc(self_summed, 1)

            first_layer_hidden(1)
            first_layer_out(0)
            first_layer_hidden(2)
            first_layer_out(1)
            first_layer_hidden(3)
            first_layer_out(2)
            first_layer_out(3)
            turn_h2(0)
            pe.wait_ge(o2_taken, 4)
            for k in range(FT):
                last = mm(bank[3][:, 0:D], ones32, neigh_t[:, k, :], start=(k == 0), stop=(k == FT - 1))
            last.then_inc(wsum_summed, 1)
            turn_h2(1)
            pe.wait_ge(wsum_ready, 1)
            for c in range(2):
                sum_neighbours(c)
            own_term(0)
            for c in range(2, CHUNKS):
                turn_h2(c)
                sum_neighbours(c)
            for c in range(1, CHUNKS):
                own_term(c)


_INS = ['x', 'adj', 'L0_gnn_in_W', 'L0_gnn_in_b', 'L0_gnn_out_W', 'L0_gnn_out_b', 'L0_gnn_r_W', 'L0_gnn_r_b',
        'L0_gnn_z_W', 'L0_gnn_z_b', 'L0_gnn_h_W', 'L0_gnn_h_b', 'L0_gnn_o1_W', 'L0_gnn_o1_b', 'L0_gnn_o2_W',
        'L0_gnn_o2_b', 'L1_gnn_w_self', 'L1_gnn_w_neigh']


def kernel(**inputs):
    import numpy as np
    import concourse.bacc as bacc
    from concourse.bass_utils import run_bass_kernel_spmd

    nc = bacc.Bacc("TRN2", target_bir_lowering=False, num_devices=1)
    arrays, args = {}, []
    for name in _INS:
        a = np.ascontiguousarray(inputs[name])
        arrays[name + "_dram"] = a
        args.append(nc.dram_tensor(name + "_dram", a.shape, mybir.dt.from_np(a.dtype), kind="ExternalInput").ap())
    out = nc.dram_tensor("out_dram", (N, D), F32, kind="ExternalOutput").ap()
    gnn_kernel(nc, *args, out)
    r = run_bass_kernel_spmd(nc, [arrays], core_ids=[0])
    return r.results[0]["out_dram"]
```
